# Optimizing a Trainium2 kernel written in Bass

```python
import numpy as np
import jax
import jax.numpy as jnp

def _softmax(x, axis=-1):
    return jax.nn.softmax(x, axis=axis)

def _gelu(x):
    return jax.nn.gelu(x, approximate=True)

def _silu(x):
    return jax.nn.silu(x)

def _sigmoid(x):
    return jax.nn.sigmoid(x)

def _layernorm(x, axis=-1, eps=1e-05):
    m = jnp.mean(x, axis=axis, keepdims=True)
    v = jnp.var(x, axis=axis, keepdims=True)
    return (x - m) / jnp.sqrt(v + eps)

def _scatter_add(tgt, idx, src, axis=0):
    return tgt.at[idx].add(src)

def _segment_sum(src, seg, n):
    return jax.ops.segment_sum(src, seg, n)
kernel_name = 'mk_metaformer_d2_conv_nchw128_r2_4f5443'

def setup_inputs(seed: int=0):
    np.random.seed(seed)
    _w = jnp.asarray

    def _rec_inputs():
        import jax
        import jax.numpy as jnp
        _gk = jax.random.key(seed)
        x = -0.0001142 + 0.9999 * jax.random.normal(jax.random.fold_in(_gk, 1), (16, 64, 36, 100), jnp.float32)
        return x
    x = _rec_inputs()

    def _L0_conv_setup():
        import jax, jax.numpy as jnp
        import numpy as np
        B, C, H, W = (16, 64, 36, 100)
        K, PAD = (9, 4)

        def conv1d(x, w):
            return jax.lax.conv_general_dilated(x, w, window_strides=(1,), padding=[(PAD, PAD)], dimension_numbers=('NCH', 'OIH', 'NCH'))

        def sweep_fwd(seq, w):

            def step(carry, row):
                new = row + jax.nn.relu(conv1d(carry, w))
                return (new, new)
            _, out = jax.lax.scan(step, seq[0], seq[1:])
            return jnp.concatenate([seq[:1], out], axis=0)

        def sweep_bwd(seq, w):
            rev = seq[::-1]

            def step(carry, row):
                new = row + jax.nn.relu(conv1d(carry, w))
                return (new, new)
            _, out = jax.lax.scan(step, rev[0], rev[1:-1])
            return jnp.concatenate([seq[:1], out[::-1], seq[-1:]], axis=0)
        key = jax.random.key(seed)
        kx, kd, ku, kr, kl = jax.random.split(key, 5)
        s = 0.03
        return {'x': jax.random.normal(kx, (B, C, H, W), jnp.float32), 'w_d': jax.random.normal(kd, (C, C, 1, K), jnp.float32) * s, 'w_u': jax.random.normal(ku, (C, C, 1, K), jnp.float32) * s, 'w_r': jax.random.normal(kr, (C, C, K, 1), jnp.float32) * s, 'w_l': jax.random.normal(kl, (C, C, K, 1), jnp.float32) * s}
    _L0_conv_all = _L0_conv_setup()
    _L0_conv_in = {k: v for k, v in _L0_conv_all.items() if k in ('w_d', 'w_u', 'w_r', 'w_l')}
    del _L0_conv_all

    def _L0_ffn_setup():
        import jax, jax.numpy as jnp
        import numpy as np
        B, S, D, E, H, O, K = (256, 1024, 64, 32, 256, 64, 8)
        key = jax.random.key(seed)
        k0, k1, k2, k3 = jax.random.split(key, 4)
        x = jax.random.normal(k0, (B, S, D), dtype=jnp.float32)
        gate_w = jax.random.normal(k1, (E, D), dtype=jnp.float32) * (1.0 / np.sqrt(D))
        gate_b = jnp.zeros((E,), dtype=jnp.float32)
        weight1 = jax.random.uniform(k2, (E, D + 1, H), dtype=jnp.float32, minval=-1.0, maxval=1.0) * (1.0 / np.sqrt(D + 1))
        weight2 = jax.random.uniform(k3, (E, H + 1, O), dtype=jnp.float32, minval=-1.0, maxval=1.0) * (1.0 / np.sqrt(H + 1))
        return {'x': x, 'gate_w': gate_w, 'gate_b': gate_b, 'weight1': weight1, 'weight2': weight2}
    _L0_ffn_all = _L0_ffn_setup()
    _L0_ffn_in = {k: v for k, v in _L0_ffn_all.items() if k in ('gate_w', 'gate_b', 'weight1', 'weight2')}
    del _L0_ffn_all

    def _L1_conv_setup():
        import jax, jax.numpy as jnp
        import numpy as np
        B, C, H, W = (16, 64, 36, 100)
        K, PAD = (9, 4)

        def conv1d(x, w):
            return jax.lax.conv_general_dilated(x, w, window_strides=(1,), padding=[(PAD, PAD)], dimension_numbers=('NCH', 'OIH', 'NCH'))

        def sweep_fwd(seq, w):

            def step(carry, row):
                new = row + jax.nn.relu(conv1d(carry, w))
                return (new, new)
            _, out = jax.lax.scan(step, seq[0], seq[1:])
            return jnp.concatenate([seq[:1], out], axis=0)

        def sweep_bwd(seq, w):
            rev = seq[::-1]

            def step(carry, row):
                new = row + jax.nn.relu(conv1d(carry, w))
                return (new, new)
            _, out = jax.lax.scan(step, rev[0], rev[1:-1])
            return jnp.concatenate([seq[:1], out[::-1], seq[-1:]], axis=0)
        key = jax.random.key(seed)
        kx, kd, ku, kr, kl = jax.random.split(key, 5)
        s = 0.03
        return {'x': jax.random.normal(kx, (B, C, H, W), jnp.float32), 'w_d': jax.random.normal(kd, (C, C, 1, K), jnp.float32) * s, 'w_u': jax.random.normal(ku, (C, C, 1, K), jnp.float32) * s, 'w_r': jax.random.normal(kr, (C, C, K, 1), jnp.float32) * s, 'w_l': jax.random.normal(kl, (C, C, K, 1), jnp.float32) * s}
    _L1_conv_all = _L1_conv_setup()
    _L1_conv_in = {k: v for k, v in _L1_conv_all.items() if k in ('w_d', 'w_u', 'w_r', 'w_l')}
    del _L1_conv_all

    def _L1_ffn_setup():
        import jax, jax.numpy as jnp
        import numpy as np
        BN_EPS = 1e-05
        key = jax.random.key(seed)
        k1, k2, k3 = jax.random.split(key, 3)
        B, T, I, H = (32, 1024, 64, 64)
        x = jax.random.normal(k1, (B, T, I), dtype=jnp.float32)
        W = jax.random.normal(k2, (H, I), dtype=jnp.float32) * (1.0 / np.sqrt(I))
        V = jnp.linalg.qr(jax.random.normal(k3, (H, H), dtype=jnp.float32))[0]
        gamma = jnp.ones((H,), dtype=jnp.float32)
        beta = jnp.zeros((H,), dtype=jnp.float32)
        return {'x': x, 'W': W, 'V': V, 'gamma': gamma, 'beta': beta}
    _L1_ffn_all = _L1_ffn_setup()
    _L1_ffn_in = {k: v for k, v in _L1_ffn_all.items() if k in ('W', 'V', 'gamma', 'beta')}
    del _L1_ffn_all
    return {'x': x, 'L0_conv_w_d': _L0_conv_in['w_d'], 'L0_conv_w_u': _L0_conv_in['w_u'], 'L0_conv_w_r': _L0_conv_in['w_r'], 'L0_conv_w_l': _L0_conv_in['w_l'], 'L0_ffn_gate_w': _L0_ffn_in['gate_w'], 'L0_ffn_gate_b': _L0_ffn_in['gate_b'], 'L0_ffn_weight1': _L0_ffn_in['weight1'], 'L0_ffn_weight2': _L0_ffn_in['weight2'], 'L1_conv_w_d': _L1_conv_in['w_d'], 'L1_conv_w_u': _L1_conv_in['w_u'], 'L1_conv_w_r': _L1_conv_in['w_r'], 'L1_conv_w_l': _L1_conv_in['w_l'], 'L1_ffn_W': _L1_ffn_in['W'], 'L1_ffn_V': _L1_ffn_in['V'], 'L1_ffn_gamma': _L1_ffn_in['gamma'], 'L1_ffn_beta': _L1_ffn_in['beta']}

def reference(x, L0_conv_w_d, L0_conv_w_u, L0_conv_w_r, L0_conv_w_l, L0_ffn_gate_w, L0_ffn_gate_b, L0_ffn_weight1, L0_ffn_weight2, L1_conv_w_d, L1_conv_w_u, L1_conv_w_r, L1_conv_w_l, L1_ffn_W, L1_ffn_V, L1_ffn_gamma, L1_ffn_beta):
    import jax
    import jax.numpy as jnp

    def _L0_conv_ref(x, w_d, w_u, w_r, w_l):
        import jax, jax.numpy as jnp
        import numpy as np
        B, C, H, W = (16, 64, 36, 100)
        K, PAD = (9, 4)

        def conv1d(x, w):
            return jax.lax.conv_general_dilated(x, w, window_strides=(1,), padding=[(PAD, PAD)], dimension_numbers=('NCH', 'OIH', 'NCH'))

        def sweep_fwd(seq, w):

            def step(carry, row):
                new = row + jax.nn.relu(conv1d(carry, w))
                return (new, new)
            _, out = jax.lax.scan(step, seq[0], seq[1:])
            return jnp.concatenate([seq[:1], out], axis=0)

        def sweep_bwd(seq, w):
            rev = seq[::-1]

            def step(carry, row):
                new = row + jax.nn.relu(conv1d(carry, w))
                return (new, new)
            _, out = jax.lax.scan(step, rev[0], rev[1:-1])
            return jnp.concatenate([seq[:1], out[::-1], seq[-1:]], axis=0)
        wd = w_d[:, :, 0, :]
        wu = w_u[:, :, 0, :]
        wr = w_r[:, :, :, 0]
        wl = w_l[:, :, :, 0]
        rows = jnp.transpose(x, (2, 0, 1, 3))
        rows = sweep_fwd(rows, wd)
        rows = sweep_bwd(rows, wu)
        x = jnp.transpose(rows, (1, 2, 0, 3))
        cols = jnp.transpose(x, (3, 0, 1, 2))
        cols = sweep_fwd(cols, wr)
        cols = sweep_bwd(cols, wl)
        return jnp.transpose(cols, (1, 2, 3, 0))

    def _L0_ffn_ref(x, gate_w, gate_b, weight1, weight2):
        import jax, jax.numpy as jnp
        import numpy as np
        B, S, D, E, H, O, K = (256, 1024, 64, 32, 256, 64, 8)
        Bn, Sn, Dn = x.shape
        logits = jnp.einsum('bsd,ed->bse', x, gate_w) + gate_b
        probs = jax.nn.softmax(logits, axis=1)
        vals, idx = jax.lax.top_k(probs.transpose(0, 2, 1), K)
        topv = vals.transpose(0, 2, 1)
        topi = idx.transpose(0, 2, 1)
        flat_idx = topi.reshape(Bn, K * E)
        gathered = jnp.take_along_axis(x, flat_idx[:, :, None], axis=1)
        gathered = gathered.reshape(Bn, K, E, Dn)
        pooled = jnp.einsum('bked,bke->bed', gathered, topv)
        ones = jnp.ones((E, Bn, 1), dtype=x.dtype)
        h = jnp.concatenate([pooled.transpose(1, 0, 2), ones], axis=-1)
        h = jax.nn.gelu(jnp.einsum('ebd,edh->ebh', h, weight1), approximate=False)
        h = jnp.concatenate([h, ones], axis=-1)
        out = jnp.einsum('ebh,eho->ebo', h, weight2)
        out = out.transpose(1, 0, 2)
        weighted = jnp.einsum('beo,bke->bkeo', out, topv).reshape(Bn, K * E, O)
        outputs = jnp.zeros((Bn, Sn, O), dtype=x.dtype)
        outputs = outputs.at[jnp.arange(Bn)[:, None], flat_idx].add(weighted)
        return outputs

    def _L1_conv_ref(x, w_d, w_u, w_r, w_l):
        import jax, jax.numpy as jnp
        import numpy as np
        B, C, H, W = (16, 64, 36, 100)
        K, PAD = (9, 4)

        def conv1d(x, w):
            return jax.lax.conv_general_dilated(x, w, window_strides=(1,), padding=[(PAD, PAD)], dimension_numbers=('NCH', 'OIH', 'NCH'))

        def sweep_fwd(seq, w):

            def step(carry, row):
                new = row + jax.nn.relu(conv1d(carry, w))
                return (new, new)
            _, out = jax.lax.scan(step, seq[0], seq[1:])
            return jnp.concatenate([seq[:1], out], axis=0)

        def sweep_bwd(seq, w):
            rev = seq[::-1]

            def step(carry, row):
                new = row + jax.nn.relu(conv1d(carry, w))
                return (new, new)
            _, out = jax.lax.scan(step, rev[0], rev[1:-1])
            return jnp.concatenate([seq[:1], out[::-1], seq[-1:]], axis=0)
        wd = w_d[:, :, 0, :]
        wu = w_u[:, :, 0, :]
        wr = w_r[:, :, :, 0]
        wl = w_l[:, :, :, 0]
        rows = jnp.transpose(x, (2, 0, 1, 3))
        rows = sweep_fwd(rows, wd)
        rows = sweep_bwd(rows, wu)
        x = jnp.transpose(rows, (1, 2, 0, 3))
        cols = jnp.transpose(x, (3, 0, 1, 2))
        cols = sweep_fwd(cols, wr)
        cols = sweep_bwd(cols, wl)
        return jnp.transpose(cols, (1, 2, 3, 0))

    def _L1_ffn_ref(x, W, V, gamma, beta):
        import jax, jax.numpy as jnp
        import numpy as np
        BN_EPS = 1e-05
        B, T, H = (x.shape[0], x.shape[1], W.shape[0])
        Wx = jnp.einsum('bti,hi->bth', x, W)
        flat = Wx.reshape(B * T, H)
        mean = jnp.mean(flat, axis=0)
        var = jnp.var(flat, axis=0)
        Wx = ((flat - mean) * jax.lax.rsqrt(var + BN_EPS) * gamma + beta).reshape(B, T, H)
        Vt = V.T

        def step(yt, wx_t):
            yt = jax.nn.sigmoid(wx_t + yt @ Vt)
            return (yt, yt)
        y0 = jnp.zeros((B, H), dtype=Wx.dtype)
        _, ys = jax.lax.scan(step, y0, jnp.swapaxes(Wx, 0, 1))
        return jnp.swapaxes(ys, 0, 1)

    def _gn(v, G=32, eps=1e-05):
        B_, C_, H_, W_ = v.shape
        g = v.reshape(B_, G, C_ // G, H_, W_)
        m = jnp.mean(g, axis=(2, 3, 4), keepdims=True)
        s = jnp.var(g, axis=(2, 3, 4), keepdims=True)
        return ((g - m) / jnp.sqrt(s + eps)).reshape(v.shape)

    def _ln_c(v, eps=1e-06):
        m = jnp.mean(v, axis=1, keepdims=True)
        s = jnp.var(v, axis=1, keepdims=True)
        return (v - m) / jnp.sqrt(s + eps)

    def _ln_t(v, eps=1e-05):
        m = jnp.mean(v, axis=-1, keepdims=True)
        s = jnp.var(v, axis=-1, keepdims=True)
        return (v - m) / jnp.sqrt(s + eps)

    def _to_tokens(v):
        B_, C_, H_, W_ = v.shape
        return v.reshape(B_, C_, H_ * W_).transpose(0, 2, 1)

    def _from_tokens(t, like):
        B_, C_, H_, W_ = like.shape
        return t.transpose(0, 2, 1).reshape(B_, C_, H_, W_)
    x = x + _L0_conv_ref(_ln_c(x), L0_conv_w_d, L0_conv_w_u, L0_conv_w_r, L0_conv_w_l)
    t = _to_tokens(x)
    t = t + _L0_ffn_ref(_ln_t(t), L0_ffn_gate_w, L0_ffn_gate_b, L0_ffn_weight1, L0_ffn_weight2)
    x = _from_tokens(t, x)
    x = x + _L1_conv_ref(_ln_c(x), L1_conv_w_d, L1_conv_w_u, L1_conv_w_r, L1_conv_w_l)
    t = _to_tokens(x)
    t = t + _L1_ffn_ref(_ln_t(t), L1_ffn_W, L1_ffn_V, L1_ffn_gamma, L1_ffn_beta)
    x = _from_tokens(t, x)
    return x

_drawn_inputs = setup_inputs


def setup_inputs(seed=0):
    import zlib

    import numpy as np

    out = dict(_drawn_inputs(seed))
    spreads = {'L0_ffn_gate_b': (0.0, 2.0), 'L1_ffn_gamma': (1.0, 0.6), 'L1_ffn_beta': (0.0, 2.0)}
    factors = {'L0_ffn_gate_w': 8.0, 'L0_ffn_weight1': 8.0, 'L0_ffn_weight2': 8.0, 'L1_ffn_V': 3.547}
    for name, (base, spread) in spreads.items():
        noise = np.random.default_rng([zlib.crc32(name.encode()), seed]).standard_normal(out[name].shape)
        drawn = base * np.exp(spread * noise) if base else spread * noise
        out[name] = jnp.asarray(drawn.astype(out[name].dtype))
    for name, factor in factors.items():
        out[name] = (out[name] * factor).astype(out[name].dtype)
    return out
```

```python
import concourse.bass as bass
from concourse import mybir
from contextlib import ExitStack

B, C, H, W = 16, 64, 36, 100
HB = B // 2
S = H * W
HP, WP = H // 2, W // 2
SLOT = S // 2
HALF = (HB + 1) * SLOT
KT = 9
OFFS = (0, -2, -1, 1, 2)
NO = len(OFFS)
CH_ROWS = 4
CH = CH_ROWS * W
NCH = H // CH_ROWS
RING = 3
E, D1, HID, D2, TOPK = 32, C + 1, 256, 257, 8
NG = 4
TC = 120
NTC = S // TC
SEG = 30
BODY = 4
EPS_C, EPS_T, EPS_BN = 1e-6, 1e-5, 1e-5


def metaformer(nc, x, conv_w, gate_w, gate_b, weight1, weight2, rnn_w, rnn_v, gamma, beta, out, t_dram, x1_dram, x2_dram):
    fp32 = mybir.dt.float32
    ALU = mybir.AluOpType
    ACT = mybir.ActivationFunctionType
    ds = bass.ds

    with ExitStack() as ctx:
        def sb(name, shape):
            return ctx.enter_context(nc.sbuf_tensor(name, shape, fp32))

        def sem(name):
            return ctx.enter_context(nc.semaphore(name))

        img = sb("img", [128, 2 * HALF])
        xl = sb("xl", [128, 2 * S])
        ring = sb("ring", [128, RING * CH])
        sq = sb("sq", [128, 2 * CH])
        rstd = sb("rstd", [128, 2 * CH])
        taps = sb("taps", [128, 4 * NO * 128])
        tt = sb("tt", [TC, 2 * 384])
        pooled = sb("pooled", [D1, B * E])
        ident = sb("ident", [128, 128])
        centre = sb("centre", [128, 128])
        average = sb("average", [128, 128])
        gate = sb("gate", [128, 2 * 128])
        gbias = sb("gbias", [128, 1])
        top8 = sb("top8", [128, TOPK])
        stat = sb("stat", [128, 8])
        lhg = sb("lhg", [128, 2 * 128])
        graw = sb("graw", [E, C])
        vt = sb("vt", [64, 64])
        wraw_r = sb("wraw_r", [64, 128])
        wbd = sb("wbd", [128, 128])
        gb = sb("gb", [64, 2])
        bns = sb("bns", [128, NG * 2 * NCH * 6])
        bnm = sb("bnm", [128, 16])
        brow = sb("brow", [1, 64])
        fold = sb("fold", [128, 128])
        warm = sb("warm", [1, 1])
        eps = sb("eps", [128, 5])
        ones = sb("ones", [1, SEG * B])
        PS = [ctx.enter_context(nc.psum_tensor(f"ps{i}", [128, 512], fp32)) for i in range(8)]

        def half(buf, h):
            return buf[h * 64:(h + 1) * 64]

        wraw = xl[:, 0:2 * C * KT]
        wt = xl[0:64, 2 * C * KT:2 * C * KT + 2 * KT * 128].rearrange("p (a k s o) -> p a k s o", a=2, k=KT, s=2)
        lh = xl[:, S:S + 2 * NG * 128]
        hidden = xl[:, S + 1024:S + 2048]
        outt = xl[0:64, S + 2048:S + 2560]
        yb = xl[0:64, 0:BODY * SEG * B].rearrange("p (s b t) -> p s b t", s=BODY, b=B)
        x2b = xl[0:64, 1920:3840].rearrange("p (b t) -> p b t", b=B)
        ob = xl[0:64, 3840:5760].rearrange("p (b t) -> p b t", b=B)
        wsc = [xl[:, 5760 + h * 64:5824 + h * 64] for h in range(2)]
        wrow = xl[0:64, 5888:5952]
        slots = img[:, :].rearrange("p (z b t) -> p z b t", z=2, b=HB + 1)

        def w1_at(e):
            z, b = [(0, 1), (0, 3), (0, 5), (0, 7), (0, 8)][e // 7]
            return slots[0:D1, z, b, (e % 7) * HID:(e % 7 + 1) * HID]

        def w2_at(c, e):
            return slots[:, 1, 1 + 2 * (2 * c + e // 16), (e % 16) * C:(e % 16 + 1) * C]

        def b2_at(e, n=1):
            if e < 16:
                return slots[0:1, 1, 8, e * C:(e + n) * C]
            return xl[0:1, S + 2560 + (e - 16) * C:S + 2560 + (e - 16 + n) * C]

        setup_dma, consts, gate_t, gate_ready = sem("setup_dma"), sem("consts"), sem("gate_t"), sem("gate_ready")
        centre_ready = sem("centre_ready")
        wdma, wtr, wcp, taps_ready = ([sem(f"{n}{l}") for l in range(2)] for n in ("wdma", "wtr", "wcp", "taps_ready"))

        class Norm:
            def __init__(self, n):
                self.loaded = [sem(f"{n}_loaded{r}") for r in range(RING)]
                self.stored = [sem(f"{n}_stored{r}") for r in range(RING)]
                self.copied = sem(f"{n}_copied")
                self.summed = sem(f"{n}_summed")
                self.centred = sem(f"{n}_centred")
                self.squared = sem(f"{n}_squared")
                self.var = sem(f"{n}_var")
                self.std = sem(f"{n}_std")
                self.rstd = sem(f"{n}_rstd")
                self.normed = sem(f"{n}_normed")
                self.mixed = sem(f"{n}_mixed")
                self.taken = sem(f"{n}_taken")
        ln = [Norm(f"ln{i}") for i in range(4)]
        state = [[sem(f"state{l}_{h}") for h in range(2)] for l in range(2)]
        conv = [[sem(f"conv{l}_{h}") for h in range(2)] for l in range(2)]

        relaid = [[sem(f"relaid{l}_{h}") for h in range(2)] for l in range(2)]
        top_max, top_found, exp_done, replaced, exp0_done, prob_diff, prob_ready = (
            sem(n) for n in ("top_max", "top_found", "exp_done", "replaced", "exp0_done", "prob_diff", "prob_ready"))
        prob_saved = sem("prob_saved")
        transposed, pool_mm, pool_read = sem("transposed"), sem("pool_mm"), sem("pool_read")
        tt_ready = [sem(f"tt_ready{j}") for j in range(2)]
        ew_dma, hid_mm, hid_act, eo_mm, outt_ready, lh_zero, lh_tr, lh_ready, lhg_ready = (
            sem(n) for n in ("ew_dma", "hid_mm", "hid_act", "eo_mm", "outt_ready", "lh_zero", "lh_tr", "lh_ready", "lhg_ready"))
        rdma, rnn_t, rnn_w_ready, bn_pe, bn_dve, bn_step, rnn_ready = (
            sem(n) for n in ("rdma", "rnn_t", "rnn_w_ready", "bn_pe", "bn_dve", "bn_step", "rnn_ready"))
        bn_std = sem("bn_std")
        pool_done = sem("pool_done")
        passed = sem("passed")
        step_mm, step_y, seg_done, x2_in, added, out_st = (
            sem(n) for n in ("step_mm", "step_y", "seg_done", "x2_in", "added", "out_st"))

        STEPS = [H - 1, H - 2, W - 1, W - 2]
        LINES0 = [1, H, 2 * H - 1, 2 * H + W - 2]
        STEPS0 = [0, H - 1, 2 * H - 3, 2 * H + W - 4]
        LINES = 2 * H + 2 * W - 4
        assert LINES == LINES0[3] + STEPS[3]

        def nat(t):
            v = t if len(t.shape) == 3 else t.rearrange("b c h w -> b c (h w)")
            return [v[h * HB:(h + 1) * HB].rearrange("b c t -> c b t") for h in range(2)]

        def nat_all(t):
            return t.rearrange("b c t -> c b t")

        def rows_view(p, h):
            return img[p[0]:p[1], h * HALF:(h + 1) * HALF].rearrange("p (b r j) -> p b r j", r=H, j=WP)

        def cols_view(p, h):
            return img[p[0]:p[1], h * HALF:(h + 1) * HALF].rearrange("p (b r j) -> p b r j", r=W, j=HP)

        LOW, HIGH, ALL = (0, 64), (64, 128), (0, 128)
        SIDE = (LOW, HIGH)

        def shape_of(k):
            rows = k < 2
            view, n, pairs = (rows_view, H, WP) if rows else (cols_view, W, HP)
            if k % 2 == 0:
                return view, int(rows), (lambda s: s), (lambda s: s + 1), pairs
            return view, int(rows), (lambda s: s * -1 + (n - 1)), (lambda s: s * -1 + (n - 2)), pairs

        SRC = [nat(x), nat(x), nat(t_dram), nat(x1_dram)]
        DST = [None, nat(t_dram), nat(x1_dram), nat(x2_dram)]
        EPS = [EPS_C, EPS_T, EPS_C, EPS_T]
        N2 = 2 * NCH
        PER = N2 // RING

        def unit(i, g, v):
            return 2 * g + v if i != 2 else g * -2 + (HB - 1 - v)

        def token_pieces(k):
            a, b = k * CH, (k + 1) * CH
            if b <= SLOT:
                return [(0, 0, a, CH)]
            if a >= SLOT:
                return [(0, 1, a - SLOT, CH)]
            return [(0, 0, a, SLOT - a), (SLOT - a, 1, 0, b - SLOT)]

        def slot_tokens(z, b, a, m):
            return slots[:, z, ds(b, 1), a:a + m].rearrange("p b t -> p (b t)")

        def whole(b):
            return slots[:, :, ds(b, 1), :].rearrange("p z b t -> p z (b t)")

        spare = slots[:, :, HB, :]

        def own(eng):
            eng.sem_inc(passed, 1)

        NIT = S // (BODY * SEG)
        HIT = NIT // 2
        block = ctx.enter_context(nc.Block())

        def sp_norm(sp, i):
            st = ln[i]
            with sp.Fori(0, NG) as g:
                units = [sp.snap(unit(i, g, v)) for v in range(2)]

                def load(n):
                    v, k, r = n // NCH, n % NCH, n % RING
                    for h in range(2):
                        sp.dma_start(half(ring, h)[:, r * CH:(r + 1) * CH],
                                     SRC[i][h][:, ds(units[v], 1), k * CH:(k + 1) * CH].rearrange("c b t -> c (b t)")
                                     ).then_inc(st.loaded[r], 16)
                for n in range(RING - 1):
                    load(n)
                for n in range(N2):
                    v, k, r = n // NCH, n % NCH, n % RING
                    if DST[i] is not None:
                        sp.wait_ge(st.summed, g * N2 + (n + 1))
                        for h in range(2):
                            sp.dma_start(DST[i][h][:, ds(units[v], 1), k * CH:(k + 1) * CH].rearrange("c b t -> c (b t)"),
                                         half(ring, h)[:, r * CH:(r + 1) * CH]).then_inc(st.stored[r], 16)
                    m = n + RING - 1
                    if m < N2:
                        if n >= 1:
                            sp.wait_ge(st.centred, g * N2 + n)
                            if DST[i] is not None:
                                sp.wait_ge(st.stored[m % RING], 32 * (g * PER + ((n - 1) // RING + 1)))
                        load(m)
                sp.wait_ge(st.centred, g * N2 + N2)
                if DST[i] is not None:
                    for r in range(RING):
                        sp.wait_ge(st.stored[r], 32 * (g * PER + PER))
                own(sp)

        def sp_taps(sp, l):
            for q in range(4):
                sp.dma_start(half(wraw, q % 2)[:, (q // 2) * C * KT:(q // 2 + 1) * C * KT],
                             conv_w[4 * l + q].rearrange("o i a b -> o (i a b)")).then_inc(wdma[l], 16)

        @block.sync
        def _(sp):
            sp.dma_start(graw[:, :], gate_w).then_inc(setup_dma, 16)
            for q in range(4):
                sp.dma_start(gbias[q * E:(q + 1) * E, :], gate_b.rearrange("(e a) -> e a", a=1)).then_inc(setup_dma, 16)
            sp_taps(sp, 0)
            sp.dma_start(wraw_r[:, 0:64], rnn_w).then_inc(rdma, 16)
            sp.dma_start(wraw_r[:, 64:128], rnn_v).then_inc(rdma, 16)
            sp.dma_start(gb[:, 0:1], gamma.rearrange("(e a) -> e a", a=1)).then_inc(rdma, 16)
            sp.dma_start(gb[:, 1:2], beta.rearrange("(e a) -> e a", a=1)).then_inc(rdma, 16)
            sp_norm(sp, 0)
            sp_norm(sp, 1)
            sp.wait_ge(pool_read, NG)
            sp.wait_ge(prob_saved, NG)
            for e0 in range(0, E, 7):
                n = min(7, E - e0)
                z, b = [(0, 1), (0, 3), (0, 5), (0, 7), (0, 8)][e0 // 7]
                sp.dma_start(slots[0:D1, z, b, 0:n * HID].rearrange("p (e h) -> p e h", e=n),
                             weight1[e0:e0 + n].rearrange("e d h -> d e h")).then_inc(ew_dma, 16)
            for c in range(2):
                for e0 in (0, 16):
                    sp.dma_start(slots[:, 1, 1 + 2 * (2 * c + e0 // 16), 0:16 * C].rearrange("p (e o) -> p e o", e=16),
                                 weight2[e0:e0 + 16, c * 128:(c + 1) * 128, :].rearrange("e p o -> p e o")).then_inc(ew_dma, 16)
            for e0 in (0, 16):
                sp.dma_start(b2_at(e0, 16).rearrange("p (e o) -> p e o", e=16),
                             weight2[e0:e0 + 16, HID:D2, :].rearrange("e p o -> p e o")).then_inc(ew_dma, 16)
            sp_taps(sp, 1)
            sp_norm(sp, 2)
            sp_norm(sp, 3)
            sp.wait_ge(rnn_ready, 1)
            with sp.Fori(0, NIT) as i:
                sp.dma_start(x2b, nat_all(x2_dram)[:, :, ds(i * (BODY * SEG), BODY * SEG)]).then_inc(x2_in, 16)
                sp.wait_ge(added, i * BODY + 2 * BODY)
                sp.dma_start(nat_all(out.rearrange("b c h w -> b c (h w)"))[:, :, ds(i * (BODY * SEG), BODY * SEG)],
                             ob).then_inc(out_st, 16)
            sp.wait_ge(out_st, 16 * (NIT + 1))

        @block.gpsimd
        def _(pool):
            done = [0]

            def alone(ins):
                done[0] += 1
                ins.then_inc(pool_done, 1)
                pool.wait_ge(pool_done, done[0])

            for buf, value in ((ident, 0.0), (average, 0.0), (fold, 0.0), (gate, 0.0), (wbd, 0.0), (taps, 0.0), (ones, 1.0),
                               (pooled, 1.0)):
                alone(pool.memset(buf[:, :], value))
            for n, value in enumerate(EPS + [EPS_BN]):
                alone(pool.memset(eps[:, n:n + 1], value))
            for h in range(2):
                alone(pool.memset(half(average, h)[:, h * 64:(h + 1) * 64], 1.0 / C))
            for base in (0, 64, -64):
                alone(pool.affine_select(out=fold[:, :], in_=fold[:, :], compare_op=ALU.not_equal, fill=0.5, base=base,
                                         pattern=[[-1, 128]], channel_multiplier=1))
            pool.affine_select(out=ident[:, :], in_=ident[:, :], compare_op=ALU.not_equal, fill=1.0, base=0,
                               pattern=[[-1, 128]], channel_multiplier=1).then_inc(consts, 1)
            with pool.Fori(0, NG) as g:
                pool.wait_ge(prob_ready, g + 1)
                own(pool)
                pool.tensor_copy(whole(2 * g), spare).then_inc(prob_saved, 1)
            pool.wait_ge(pool_read, NG)
            pool.wait_ge(prob_saved, NG)
            pool.memset(lh, 0.0).then_inc(lh_zero, 1)
            pool.wait_ge(lh_ready, 1)
            pool.tensor_copy(lhg[:, :], lh[:, (NG - 1) * 256:NG * 256]).then_inc(lhg_ready, 1)
            with pool.Fori(0, NG - 1) as g:
                pool.wait_ge(ln[2].summed, g * N2 + N2)
                own(pool)
                pool.tensor_copy(lhg[:, :], lh[:, ds(g * -256 + (NG - 2) * 256, 256)]).then_inc(lhg_ready, 1)

        def pe_taps(pe, l):
            pe.wait_ge(wdma[l], 64)
            wk = wraw.rearrange("p (a i k) -> p a k i", a=2, k=KT)
            for a in range(2):
                for k in range(KT):
                    if a == 1 and k % 4 == 0:
                        pe.wait_ge(wcp[l], k // 4 + 1)
                    last = pe.transpose(PS[4 + k // 4][0:64, (k % 4) * 128:(k % 4 + 1) * 128], wk[:, a, k, :], ident[:, :])
                    if k % 4 == 3 or k == KT - 1:
                        last.then_inc(wtr[l], 1)

        def pe_norm(pe, i, before=None, after=None, ending=None):
            st = ln[i]
            with pe.Fori(0, NG) as g:
                for n in range(N2 + 2):
                    if n < N2:
                        r = n % RING
                        if before:
                            before(g, n)
                        if i == 0:
                            pe.wait_ge(st.loaded[r], 32 * (g * PER + (n // RING + 1)))
                        else:
                            pe.wait_ge(st.summed, g * N2 + (n + 1))
                        if n >= RING:
                            pe.wait_ge(st.normed, g * N2 + (n - RING + 1))
                        pe.matmul(PS[r][:, 0:CH], centre[:, :], ring[:, r * CH:(r + 1) * CH], start=True, stop=True
                                  ).then_inc(st.centred, 1)
                    if 1 <= n <= N2:
                        m = n - 1
                        pe.wait_ge(st.squared, g * N2 + (m + 1))
                        if m >= 2:
                            pe.wait_ge(st.std, g * N2 + (m - 1))
                        pe.matmul(PS[3 + m % 2][:, 0:CH], average[:, :], sq[:, (m % 2) * CH:(m % 2 + 1) * CH],
                                  start=True, stop=True).then_inc(st.var, 1)
                    if n >= 2 and after:
                        after(g, n - 2)
                pe.wait_ge(st.normed, g * N2 + N2)
                if ending:
                    ending(g)
                own(pe)

        def pe_sweep(pe, l, k):
            view, s0, src, _, pairs = shape_of(k)
            with pe.Fori(0, STEPS[k]) as s:
                at = pe.snap(src(s))
                for h in range(2):
                    acc = PS[h][:, 0:HB * pairs].rearrange("p (b j) -> p b j", b=HB)
                    v = view(ALL, h)
                    pe.wait_ge(state[l][h], s + LINES0[k])
                    for n, d in enumerate(OFFS):
                        lo, hi = max(0, -d), min(pairs, pairs - d)
                        last = pe.matmul(acc[:, :, lo:hi], taps[:, (k * NO + d + 2) * 128:(k * NO + d + 3) * 128],
                                         v[:, s0:s0 + HB, ds(at, 1), lo + d:hi + d].rearrange("p b r j -> p b (r j)"),
                                         start=(n == 0), stop=(n == NO - 1))
                    last.then_inc(conv[l][h], 1)

        def logits(pe, g, n):
            if n < NCH:
                return
            k = n - NCH
            if k >= 2:
                pe.wait_ge(ln[1].taken, g * NCH + (k - 1))
            pe.wait_ge(ln[1].normed, g * N2 + (n + 1))
            for v in range(2):
                last = pe.matmul(PS[5 + k % 2][:, 0:CH], gate[:, v * 128:(v + 1) * 128],
                                 xl[:, v * S + k * CH:v * S + (k + 1) * CH], start=(v == 0), stop=(v == 1))
            last.then_inc(ln[1].mixed, 1)

        def pooling(pe, g):
            pe.wait_ge(prob_ready, g + 1)
            for c in range(NTC + 1):
                if c < NTC:
                    bank = PS[5 + c % 2]
                    if c >= 2:
                        pe.wait_ge(tt_ready[c % 2], g * (NTC // 2) + c // 2)
                    pe.transpose(bank[0:TC, 0:128], slots[:, c // (NTC // 2), HB, (c % (NTC // 2)) * TC:(c % (NTC // 2) + 1) * TC], ident[:, :])
                    for v in range(2):
                        last = pe.transpose(bank[0:TC, 128 + v * 128:256 + v * 128],
                                            xl[:, v * S + c * TC:v * S + (c + 1) * TC], ident[:, :])
                    last.then_inc(transposed, 1)
                if c >= 1:
                    m = c - 1
                    pe.wait_ge(tt_ready[m % 2], g * (NTC // 2) + (m // 2 + 1))
                    o = (m % 2) * 384
                    for v in range(2):
                        last = pe.matmul(PS[v][:, 0:64], tt[:, o + 128 + v * 128:o + 256 + v * 128],
                                         tt[:, o + v * 64:o + (v + 1) * 64], start=(m == 0), stop=(m == NTC - 1))
                    last.then_inc(pool_mm, 1)
            pe.wait_ge(pool_read, g + 1)

        def mixture(pe, g, n):
            v, k = n // NCH, n % NCH
            if n == 0:
                pe.wait_ge(lhg_ready, g + 1)
            if n >= 2:
                pe.wait_ge(ln[2].summed, g * N2 + (n - 1))
            for o, z, a, m in token_pieces(k):
                last = pe.matmul(PS[5 + n % 2][:, o:o + m], lhg[:, (1 - v) * 128:(2 - v) * 128],
                                 slot_tokens(z, (HB - 2) - 2 * g, a, m), start=True, stop=True)
            last.then_inc(ln[2].mixed, 1)

        def rnn_input(pe, g, n):
            v, k = n // NCH, n % NCH
            if n >= 2:
                pe.wait_ge(ln[3].taken, g * N2 + (n - 1))
            pe.wait_ge(ln[3].normed, g * N2 + (n + 1))
            for o, z, a, m in token_pieces(k):
                last = pe.matmul(PS[5 + n % 2][:, o:o + m], wbd[:, :], slot_tokens(z, 2 * g + v, a, m), start=True, stop=True)
            last.then_inc(ln[3].mixed, 1)

        def fill_bias(pe, bank, c0, w, first):
            pe.matmul(PS[bank][0:64, c0:c0 + w], brow[:, :], ones[:, c0:c0 + w], start=first, stop=False,
                      skip_group_check=True)

        def fill_input(pe, bank, h, z, t0, c0, w, last):
            acc = PS[bank][0:64, 0:SEG * B].rearrange("p (t b) -> p b t", b=B)
            tok = slots[:, ds(z, 1), 0:HB, ds(t0 + c0, w)].rearrange("p z b t -> p (z b) t")
            pe.matmul(acc[:, h * HB:(h + 1) * HB, c0:c0 + w], wsc[h], tok, start=False, stop=last, skip_group_check=True)

        @block.tensor
        def _(pe):
            pe.wait_ge(consts, 1)
            pe.wait_ge(setup_dma, 80)
            pe.transpose(PS[7][0:C, 0:E], graw[:, :], ident[0:E, 0:E]).then_inc(gate_t, 1)
            pe.wait_ge(rdma, 64)
            pe.wait_ge(gate_ready, 1)
            for a in range(2):
                last = pe.transpose(PS[7][0:64, 64 + a * 64:128 + a * 64], wraw_r[:, a * 64:(a + 1) * 64], ident[0:64, 0:64])
            last.then_inc(rnn_t, 1)
            pe_taps(pe, 0)
            pe.wait_ge(wcp[0], 6)
            pe.wait_ge(centre_ready, 1)
            pe_norm(pe, 0)
            pe.wait_ge(taps_ready[0], 1)
            for k in range(4):
                pe_sweep(pe, 0, k)
            pe.wait_ge(gate_ready, 1)
            pe_norm(pe, 1, after=lambda g, n: logits(pe, g, n), ending=lambda g: pooling(pe, g))

            pe.wait_ge(ew_dma, 16 * 11)
            pv = pooled[:, :].rearrange("p (b e) -> p e b", e=E)
            for e in range(E):
                for c in range(2):
                    last = pe.matmul(PS[e // 16][:, (e % 16) * 32 + c * 16:(e % 16) * 32 + (c + 1) * 16],
                                     w1_at(e)[:, c * 128:(c + 1) * 128], pv[:, e, :], start=True, stop=True)
                if e % 16 == 15:
                    last.then_inc(hid_mm, 1)
            eo = PS[2][0:64, :].rearrange("p (b e) -> p e b", e=E)
            for e in range(E):
                if e % 16 == 0:
                    pe.wait_ge(hid_act, e // 16 + 1)
                for c in range(2):
                    pe.matmul(eo[:, e, :], w2_at(c, e), hidden[:, e * 32 + c * 16:e * 32 + (c + 1) * 16],
                              start=(c == 0), stop=False)
                last = pe.matmul(eo[:, e, :], b2_at(e), ones[:, 0:B], start=False, stop=True)
            last.then_inc(eo_mm, 1)
            pe.wait_ge(outt_ready, 1)
            for g in range(NG):
                last = pe.transpose(PS[3][:, g * 64:(g + 1) * 64], outt[:, g * 128:(g + 1) * 128], ident[0:64, 0:64])
            last.then_inc(lh_tr, 1)
            pe_taps(pe, 1)
            pe.wait_ge(wcp[1], 6)
            pe_norm(pe, 2, before=lambda g, n: mixture(pe, g, n))
            pe.wait_ge(taps_ready[1], 1)
            for k in range(4):
                pe_sweep(pe, 1, k)
            pe.wait_ge(rnn_w_ready, 1)
            pe_norm(pe, 3, after=lambda g, n: rnn_input(pe, g, n))

            pe.wait_ge(bn_dve, 1)
            pe.matmul(PS[7][:, 0:1], fold[:, :], bnm[:, 0:1], start=True, stop=True).then_inc(bn_pe, 1)
            pe.wait_ge(bn_dve, 2)
            pe.matmul(PS[7][:, 2:3], fold[:, :], bnm[:, 3:4], start=True, stop=True).then_inc(bn_pe, 1)
            pe.wait_ge(bn_dve, 3)
            pe.transpose(PS[7][0:64, 64:128], wrow, ident[0:64, 0:64])
            pe.transpose(PS[7][0:1, 128:192], bnm[0:64, 8:9], ident[0:64, 0:64]).then_inc(bn_pe, 1)
            pe.wait_ge(rnn_ready, 1)

            with pe.Fori(0, 2) as z:
                with pe.Fori(0, HIT) as j:
                    t0 = j * (BODY * SEG)
                    fill_bias(pe, 0, 0, SEG * B, True)
                    for h in range(2):
                        fill_input(pe, 0, h, z, t0, 0, SEG, h == 1)
                    for s in range(BODY):
                        for t in range(SEG):
                            n = s * SEG + t
                            if n == 0:
                                pe.wait_ge(step_y, BODY * SEG)
                                pe.sem_clear(step_y)
                            else:
                                pe.wait_ge(step_y, n)
                            if t == 0:
                                pe.sem_inc(seg_done, 1)
                            prev = yb[:, s, :, t - 1] if t else yb[:, (s - 1) % BODY, :, SEG - 1]
                            pe.matmul(PS[s % 2][0:64, t * B:(t + 1) * B], vt[:, :], prev, start=False, stop=True,
                                      skip_group_check=True).then_inc(step_mm, 1)
                            if s < BODY - 1 and t < 15:
                                if t < 5:
                                    fill_bias(pe, (s + 1) % 2, t * 96, 96, t == 0)
                                else:
                                    h, c = (t - 5) // 5, (t - 5) % 5
                                    fill_input(pe, (s + 1) % 2, h, z, t0 + (s + 1) * SEG, c * 6, 6, t == 14)
            pe.wait_ge(step_y, BODY * SEG)
            pe.sem_inc(seg_done, 1)

        def act_relayout(act, l):
            relayout(act, l, 1, lambda o, a: act.activation(o, a, ACT.Copy))

        def relayout(eng, l, h, move):
            eng.wait_ge(state[l][h], LINES0[2] - 1)
            eng.sem_inc(relaid[l][h], 1)
            with eng.Fori(0, HB) as b:
                eng.wait_ge(relaid[l][h], b + 1)
                own(eng)
                for hp in range(2):
                    for wp in range(2):
                        dst = cols_view(SIDE[hp], h)[:, ds(b, 1), wp::2, :].rearrange("p b w j -> p (b w) j")
                        src = rows_view(SIDE[wp], h)[:, ds(b + 1, 1), hp::2, :].rearrange("p b r j -> p j (b r)")
                        last = move(dst, src)
                last.then_inc(relaid[l][h], 1)
            eng.wait_ge(relaid[l][h], HB + 1)
            eng.sem_inc(state[l][h], 1)

        def act_norm(act, i, copy=False, later=None, ending=None):
            st = ln[i]
            with act.Fori(0, NG) as g:
                def natural(v, piece):
                    h, hp = piece // 2, piece % 2
                    dst = half(xl, h)[:, v * S:(v + 1) * S].rearrange("p (r w) -> p r w", w=W)[:, hp::2, :]
                    src = cols_view(SIDE[hp], h)[:, ds(unit(i, g, v), 1), :, :].rearrange("p b w j -> p j (b w)")
                    ins = act.activation(dst, src, ACT.Copy)
                    if piece == 3:
                        ins.then_inc(st.copied, 1)
                if copy:
                    for piece in range(4):
                        natural(0, piece)
                for n in range(N2 + 1):
                    if n < N2:
                        act.wait_ge(st.centred, g * N2 + (n + 1))
                        if n >= 2:
                            act.wait_ge(st.var, g * N2 + (n - 1))
                        act.activation(sq[:, (n % 2) * CH:(n % 2 + 1) * CH], PS[n % RING][:, 0:CH], ACT.Square
                                       ).then_inc(st.squared, 1)
                    if n >= 1:
                        m = n - 1
                        act.wait_ge(st.var, g * N2 + (m + 1))
                        if m >= 2:
                            act.wait_ge(st.normed, g * N2 + (m - 1))
                        act.activation(rstd[:, (m % 2) * CH:(m % 2 + 1) * CH], PS[3 + m % 2][:, 0:CH], ACT.Sqrt,
                                       bias=eps[:, i:i + 1]).then_inc(st.std, 1)
                    if copy and n in (1, 3, 5, 7):
                        natural(1, n // 2)
                    if later and n < N2:
                        later(g, n)
                if ending:
                    ending(g)

        def take_logits(act, g, k):
            act.wait_ge(ln[1].mixed, g * NCH + (k + 1))
            for o, z, a, m in token_pieces(k):
                last = act.activation(spare[:, z, a:a + m], PS[5 + k % 2][:, o:o + m], ACT.Identity, bias=gbias[:, 0:1])
            last.then_inc(ln[1].taken, 1)

        def route(act, g):
            for k in range(NCH - 2, NCH):
                take_logits(act, g, k)
            act.wait_ge(top_found, g + 1)
            own(act)
            act.activation(whole(2 * g), spare, ACT.Exp, bias=stat[:, 0:1], accum_out=stat[:, 1:2]).then_inc(exp_done, 1)
            act.wait_ge(replaced, g + 1)
            act.activation(spare, spare, ACT.Exp, bias=stat[:, 0:1]).then_inc(exp0_done, 1)
            for c in range(1, NTC, 2):
                take_transposed(act, g, c, lambda o, a: act.activation(o, a, ACT.Copy))
            act.wait_ge(pool_mm, g * NTC + NTC)
            for v in range(2):
                for h in range(2):
                    last = act.activation(pooled[0:C, ds(g * 128 + (2 * v + h) * E, E)],
                                          half(PS[v], h)[:, h * E:(h + 1) * E], ACT.Copy)
            last.then_inc(pool_read, 1)
            act.wait_ge(prob_saved, g + 1)
            own(act)

        def take_transposed(eng, g, c, move):
            eng.wait_ge(transposed, g * NTC + (c + 1))
            if c >= 2:
                eng.wait_ge(pool_mm, g * NTC + (c - 1))
            move(tt[:, (c % 2) * 384:(c % 2 + 1) * 384], PS[5 + c % 2][0:TC, 0:384]).then_inc(tt_ready[c % 2], 1)

        @block.scalar
        def _(act):
            act.wait_ge(setup_dma, 80)
            act.wait_ge(consts, 1)
            act_norm(act, 0)
            act_relayout(act, 0)
            for h in range(2):
                act.wait_ge(state[0][h], LINES)
            act_norm(act, 1, copy=True,
                     later=lambda g, n: take_logits(act, g, n - NCH - 2) if n >= NCH + 2 else None,
                     ending=lambda g: route(act, g))
            for j in range(2):
                act.wait_ge(hid_mm, j + 1)
                act.activation(hidden[:, j * 512:(j + 1) * 512], PS[j][:, :], ACT.Gelu).then_inc(hid_act, 1)
            act_norm(act, 2)
            act_relayout(act, 1)
            for h in range(2):
                act.wait_ge(state[1][h], LINES)
            act_norm(act, 3, copy=True)
            act.wait_ge(bn_pe, 2)
            act.activation(bnm[0:64, 4:5], PS[7][0:64, 2:3], ACT.Sqrt, bias=eps[0:64, 4:5]).then_inc(bn_std, 1)
            act.wait_ge(rnn_ready, 1)
            act.activation(warm[:, :], ones[0:1, 0:1], ACT.Sigmoid)
            with act.Fori(0, NIT) as i:
                for s in range(BODY):
                    act.wait_ge(added, i * BODY + (s + 1))
                    for t in range(SEG):
                        n = s * SEG + t
                        act.wait_ge(step_mm, n + 1)
                        if n == BODY * SEG - 1:
                            act.sem_clear(step_mm)
                        act.activation(yb[:, s, :, t], PS[s % 2][0:64, t * B:(t + 1) * B], ACT.Sigmoid).then_inc(step_y, 1)

        def dve_taps(dve, l):
            for a in range(2):
                for j, (k0, k1) in enumerate(((0, 4), (4, 8), (8, 9))):
                    dve.wait_ge(wtr[l], a * 3 + j + 1)
                    dve.tensor_copy(wt[:, a, k0:k1, :, :],
                                    PS[4 + j][0:64, 0:(k1 - k0) * 128].rearrange("p (k s o) -> p k s o", s=2, o=64)
                                    ).then_inc(wcp[l], 1)

            dve.wait_ge(wcp[l], 6)
            for q in range(4):
                for ip in range(2):
                    for op in range(2):
                        d0, d1 = (-2, 2) if ip == op else (-1, 2) if ip < op else (-2, 1)
                        k0 = 2 * d0 + 4 + ip - op
                        dst = half(taps, ip)[:, q * NO * 128:(q + 1) * NO * 128].rearrange("p (d o c) -> p d o c", d=NO, o=2)
                        last = dve.tensor_copy(dst[:, d0 + 2:d1 + 3, op, :], wt[:, q // 2, k0:k0 + 2 * (d1 - d0) + 1:2, q % 2, :])
            last.then_inc(taps_ready[l], 1)

        def dve_norm(dve, i, later=None, ending=None):
            st = ln[i]
            with dve.Fori(0, NG) as g:
                units = [dve.snap(unit(i, g, v) + 1) for v in range(2)]
                for n in range(N2 + 2):
                    if n < N2 and i > 0:
                        v, k, r = n // NCH, n % NCH, n % RING
                        rc = ring[:, r * CH:(r + 1) * CH]
                        dve.wait_ge(st.loaded[r], 32 * (g * PER + (n // RING + 1)))
                        if i == 2:
                            dve.wait_ge(st.mixed, g * N2 + (n + 1))
                            add = PS[5 + n % 2][:, 0:CH]
                        else:
                            dve.wait_ge(st.copied, g * 2 + (v + 1))
                            add = xl[:, v * S + k * CH:v * S + (k + 1) * CH]
                        dve.tensor_tensor(rc, add, rc, ALU.add).then_inc(st.summed, 1)
                    if 1 <= n <= N2:
                        m = n - 1
                        v, k, r = m // NCH, m % NCH, m % RING
                        dve.wait_ge(st.std, g * N2 + (m + 1))
                        rs = rstd[:, (m % 2) * CH:(m % 2 + 1) * CH]
                        dve.reciprocal(rs, rs).then_inc(st.rstd, 1)
                        dve.wait_ge(st.rstd, g * N2 + (m + 1))
                        if i in (0, 2):
                            for h in range(2):
                                for wp in range(2):
                                    dst = rows_view(SIDE[wp], h)[:, ds(units[v], 1), k * CH_ROWS:(k + 1) * CH_ROWS, :]
                                    pick = (lambda t: half(t, h).rearrange("p (r j e) -> p r j e", j=WP, e=2)[:, :, :, wp])
                                    last = dve.tensor_tensor(dst.rearrange("p b r j -> p (b r) j"), pick(PS[r][:, 0:CH]), pick(rs),
                                                             ALU.mult)
                        elif i == 1:
                            last = dve.tensor_tensor(xl[:, v * S + k * CH:v * S + (k + 1) * CH], PS[r][:, 0:CH], rs, ALU.mult)
                        else:
                            for o, z, a, c in token_pieces(k):
                                last = dve.tensor_tensor(slot_tokens(z, 2 * g + v, a, c), PS[r][:, o:o + c], rs[:, o:o + c], ALU.mult)
                        last.then_inc(st.normed, 1)
                    if n >= 2 and later:
                        later(g, n - 2)
                if ending:
                    ending(g)

        def dve_route(dve, g):
            dve.wait_ge(ln[1].taken, g * NCH + NCH)
            own(dve)
            dve.max(top8[:, :], spare).then_inc(top_max, 1)
            dve.wait_ge(top_max, g + 1)
            dve.tensor_scalar(stat[:, 0:1], top8[:, 0:1], -1.0, None, ALU.mult).then_inc(top_found, 1)
            dve.wait_ge(exp_done, g + 1)
            own(dve)
            dve.match_replace(spare, top8[:, :], spare, -1e30).then_inc(replaced, 1)
            dve.reciprocal(stat[:, 2:3], stat[:, 1:2])
            dve.wait_ge(exp0_done, g + 1)
            dve.tensor_tensor(spare, whole(2 * g), spare, ALU.subtract).then_inc(prob_diff, 1)
            dve.wait_ge(prob_diff, g + 1)
            dve.tensor_scalar(spare, spare, stat[:, 2:3], None, ALU.mult).then_inc(prob_ready, 1)
            for c in range(0, NTC, 2):
                take_transposed(dve, g, c, lambda o, a: dve.tensor_copy(o, a))

        def dve_sweep(dve, l, k):
            view, s0, _, target, pairs = shape_of(k)
            with dve.Fori(0, STEPS[k]) as s:
                at = dve.snap(target(s))
                for h in range(2):
                    acc = PS[h][:, 0:HB * pairs].rearrange("p (b j) -> p b j", b=HB)
                    line = view(ALL, h)[:, s0:s0 + HB, ds(at, 1), :].rearrange("p b r j -> p b (r j)")
                    dve.wait_ge(conv[l][h], s + (STEPS0[k] + 1))
                    dve.scalar_tensor_tensor(out=line, in0=acc, scalar=0.0, in1=line, op0=ALU.max, op1=ALU.add
                                             ).then_inc(state[l][h], 1)

        def dve_layer(dve, l):
            dve.wait_ge(ln[2 * l].normed, NG * N2)
            for h in range(2):
                dve.sem_inc(state[l][h], 1)
            dve_sweep(dve, l, 0)
            dve_sweep(dve, l, 1)
            relayout(dve, l, 0, lambda o, a: dve.tensor_copy(o, a))
            dve_sweep(dve, l, 2)
            dve_sweep(dve, l, 3)

        def bn_take(dve, g, n):
            dve.wait_ge(ln[3].mixed, g * N2 + (n + 1))
            dve.bn_stats(bns[:, ds(g * (N2 * 6) + n * 6, 6)], PS[5 + n % 2][:, 0:CH]).then_inc(ln[3].taken, 1)

        @block.vector
        def _(dve):
            dve.wait_ge(consts, 1)
            dve.tensor_tensor(centre[:, :], ident[:, :], average[:, :], ALU.subtract).then_inc(centre_ready, 1)
            dve.wait_ge(gate_t, 1)
            for v in range(2):
                for h in range(2):
                    c0 = v * 128 + v * 64 + h * E
                    last = dve.tensor_copy(half(gate, h)[:, c0:c0 + E], PS[7][0:C, 0:E])
            last.then_inc(gate_ready, 1)
            dve.wait_ge(rnn_t, 1)
            for h in range(2):
                dve.tensor_copy(half(wbd, h)[:, h * 64:(h + 1) * 64], PS[7][0:64, 64:128])
            dve.tensor_copy(vt[:, :], PS[7][0:64, 128:192]).then_inc(rnn_w_ready, 1)
            dve_taps(dve, 0)
            dve_norm(dve, 0)
            dve_layer(dve, 0)
            dve_norm(dve, 1, ending=lambda g: dve_route(dve, g))
            dve.wait_ge(eo_mm, 1)
            dve.tensor_copy(outt, PS[2][0:64, :]).then_inc(outt_ready, 1)
            dve.wait_ge(lh_zero, 1)
            dve.wait_ge(lh_tr, 1)
            for g in range(NG):
                for v in range(2):
                    for h in range(2):
                        p, c0 = v * 64 + h * E, (2 * g + v) * 128 + h * 64
                        last = dve.tensor_copy(lh[p:p + E, c0:c0 + 64], PS[3][p:p + E, g * 64:(g + 1) * 64])
            last.then_inc(lh_ready, 1)
            dve_taps(dve, 1)
            dve_norm(dve, 2)
            dve_layer(dve, 1)
            dve_norm(dve, 3, later=lambda g, n: bn_take(dve, g, n))

            def link(ins, n):
                ins.then_inc(bn_step, 1)
                dve.wait_ge(bn_step, n)
            dve.wait_ge(ln[3].taken, NG * N2)
            dve.bn_aggr(bnm[:, 0:2], bns[:, :]).then_inc(bn_dve, 1)
            dve.wait_ge(bn_pe, 1)
            link(dve.tensor_tensor(bnm[:, 2:3], bnm[:, 0:1], PS[7][:, 0:1], ALU.subtract), 1)
            dve.scalar_tensor_tensor(out=bnm[:, 3:4], in0=bnm[:, 2:3], scalar=bnm[:, 2:3], in1=bnm[:, 1:2],
                                     op0=ALU.mult, op1=ALU.add).then_inc(bn_dve, 1)
            dve.wait_ge(bn_std, 1)
            link(dve.reciprocal(bnm[0:64, 5:6], bnm[0:64, 4:5]), 2)
            link(dve.tensor_tensor(bnm[0:64, 6:7], bnm[0:64, 5:6], gb[:, 0:1], ALU.mult), 3)
            link(dve.tensor_tensor(bnm[0:64, 7:8], PS[7][0:64, 0:1], bnm[0:64, 6:7], ALU.mult), 4)
            link(dve.tensor_tensor(bnm[0:64, 8:9], gb[:, 1:2], bnm[0:64, 7:8], ALU.subtract), 5)
            dve.tensor_scalar(wrow, wraw_r[:, 0:64], bnm[0:64, 6:7], None, ALU.mult).then_inc(bn_dve, 1)
            for h in range(2):
                link(dve.memset(wsc[h], 0.0), 6 + h)
            dve.memset(yb[:, BODY - 1, :, SEG - 1], 0.0).then_inc(step_y, BODY * SEG)
            dve.wait_ge(bn_pe, 3)
            for h in range(2):
                dve.tensor_copy(half(wsc[h], h), PS[7][0:64, 64:128])
            dve.tensor_copy(brow[:, :], PS[7][0:1, 128:192]).then_inc(rnn_ready, 1)
            dve.sem_inc(added, BODY)
            dve.sem_inc(out_st, 16)
            with dve.Fori(0, NIT) as i:
                dve.wait_ge(x2_in, i * 16 + 16)
                dve.wait_ge(out_st, i * 16 + 16)
                for s in range(BODY):
                    dve.wait_ge(seg_done, i * BODY + (s + 2))
                    dve.tensor_tensor(ob[:, :, s * SEG:(s + 1) * SEG], x2b[:, :, s * SEG:(s + 1) * SEG], yb[:, s, :, :],
                                      ALU.add).then_inc(added, 1)


_INS = ['x', 'L0_conv_w_d', 'L0_conv_w_u', 'L0_conv_w_r', 'L0_conv_w_l', 'L0_ffn_gate_w', 'L0_ffn_gate_b', 'L0_ffn_weight1',
        'L0_ffn_weight2', 'L1_conv_w_d', 'L1_conv_w_u', 'L1_conv_w_r', 'L1_conv_w_l', 'L1_ffn_W', 'L1_ffn_V', 'L1_ffn_gamma',
        'L1_ffn_beta']
_OUTS = [((B, C, H, W), 'float32')]


def kernel(**inputs):
    import numpy as _np
    import concourse.bacc as _bacc
    from concourse import mybir as _mybir
    from concourse.bass_utils import run_bass_kernel_spmd as _run

    nc = _bacc.Bacc("TRN2", target_bir_lowering=False, num_devices=1)
    arrays, a = {}, {}
    for name in _INS:
        v = _np.ascontiguousarray(inputs[name])
        arrays[f"in_{name}_dram"] = v
        a[name] = nc.dram_tensor(f"in_{name}_dram", v.shape, _mybir.dt.from_np(v.dtype), kind="ExternalInput").ap()
    outs = [nc.dram_tensor(f"out_{i}_dram", shape, _mybir.dt.from_np(_np.dtype(dtype)), kind="ExternalOutput").ap()
            for i, (shape, dtype) in enumerate(_OUTS)]
    scratch = [nc.dram_tensor(f"{n}_dram", (B, C, S), _mybir.dt.float32, kind="Internal").ap() for n in ("t", "x1", "x2")]
    metaformer(nc, a['x'], [a[f"L{l}_conv_w_{d}"] for l in range(2) for d in "durl"], a['L0_ffn_gate_w'], a['L0_ffn_gate_b'],
               a['L0_ffn_weight1'], a['L0_ffn_weight2'], a['L1_ffn_W'], a['L1_ffn_V'], a['L1_ffn_gamma'], a['L1_ffn_beta'],
               outs[0], *scratch)
    r = _run(nc, [arrays], core_ids=[0])
    return r.results[0]["out_0_dram"]
```

```python
import concourse.bass as bass
from concourse import mybir
from contextlib import ExitStack

B, C, H, W = 16, 64, 36, 100
HB = B // 2
S = H * W
HP, WP = H // 2, W // 2
SLOT = S // 2
HALF = (HB + 1) * SLOT
KT = 9
OFFS = (0, -2, -1, 1, 2)
NO = len(OFFS)
CH_ROWS = 4
CH = CH_ROWS * W
NCH = H // CH_ROWS
RING = 3
E, D1, HID, D2, TOPK = 32, C + 1, 256, 257, 8
NG = 4
TC = 120
NTC = S // TC
SEG = 30
BODY = 4
EPS_C, EPS_T, EPS_BN = 1e-6, 1e-5, 1e-5


def metaformer(nc, x, conv_w, gate_w, gate_b, weight1, weight2, rnn_w, rnn_v, gamma, beta, out, t_dram, x1_dram, x2_dram):
    fp32 = mybir.dt.float32
    ALU = mybir.AluOpType
    ACT = mybir.ActivationFunctionType
    ds = bass.ds

    with ExitStack() as ctx:
        def sb(name, shape):
            return ctx.enter_context(nc.sbuf_tensor(name, shape, fp32))

        def sem(name):
            return ctx.enter_context(nc.semaphore(name))

        img = sb("img", [128, 2 * HALF])
        xl = sb("xl", [128, 2 * S])
        ring = sb("ring", [128, RING * CH])
        sums = sb("sums", [128, RING * CH])
        sq = sb("sq", [128, 2 * CH])
        rstd = sb("rstd", [128, CH])
        pick = sb("pick", [128, 254])
        spread = sb("spread", [128, 5 * 128])
        taps = sb("taps", [128, 4 * NO * 128])
        tt = sums[0:TC, 0:2 * 384]
        pooled = sb("pooled", [D1, B * E])
        ident = sb("ident", [128, 128])
        centre = sb("centre", [128, 128])
        average = sq[:, 0:128]
        gate = sb("gate", [128, 2 * 128])
        gbias = sb("gbias", [128, 1])
        top8 = sb("top8", [128, TOPK])
        stat = sb("stat", [128, 8])
        lhg = sb("lhg", [128, 2 * 128])
        graw = sb("graw", [E, C])
        vt = sb("vt", [65, 64])
        wraw_r = sb("wraw_r", [64, 128])
        wbd = sb("wbd", [128, 128])
        gb = sb("gb", [64, 2])
        bns = sb("bns", [128, NG * 2 * NCH * 6])
        bnm = sb("bnm", [128, 16])
        fold = sb("fold", [128, 128])
        warm = sb("warm", [1, 1])
        eps = sb("eps", [128, 5])
        ones = sb("ones", [1, B])
        PS = [ctx.enter_context(nc.psum_tensor(f"ps{i}", [128, 512], fp32)) for i in range(8)]

        def half(buf, h):
            return buf[h * 64:(h + 1) * 64]

        wraw = xl[:, 0:2 * C * KT]
        wt = xl[0:64, 2 * C * KT:2 * C * KT + 2 * KT * 128].rearrange("p (a k s o) -> p a k s o", a=2, k=KT, s=2)
        hidden = xl[:, S + 1024:S + 2048]
        outt = xl[0:64, S + 2048:S + 2560]
        yb = xl[0:65, 0:BODY * SEG * B].rearrange("p (s b t) -> p s b t", s=BODY, b=B)
        x2b = xl[0:64, 1920:3840].rearrange("p (b t) -> p b t", b=B)
        ob = xl[0:64, 3840:5760].rearrange("p (b t) -> p b t", b=B)
        wsc = [xl[:, 5760 + h * 64:5824 + h * 64] for h in range(2)]
        wrow = xl[0:64, 5888:5952]
        slots = img[:, :].rearrange("p (z b t) -> p z b t", z=2, b=HB + 1)

        lh = slots[:, 0, 1, 0:2 * NG * 128]

        def w1_at(e):
            z, b = [(0, 1), (0, 3), (0, 5), (0, 7), (0, 8)][e // 7]
            return slots[0:D1, z, b, (e % 7) * HID:(e % 7 + 1) * HID]

        def w2_at(c, e):
            return slots[:, 1, 1 + 2 * (2 * c + e // 16), (e % 16) * C:(e % 16 + 1) * C]

        def b2_at(e, n=1):
            if e < 16:
                return slots[0:1, 1, 8, e * C:(e + n) * C]
            return xl[0:1, S + 2560 + (e - 16) * C:S + 2560 + (e - 16 + n) * C]

        setup_dma, consts, gate_t, gate_ready = sem("setup_dma"), sem("consts"), sem("gate_t"), sem("gate_ready")
        centre_ready, pick_ready, spread_ready = sem("centre_ready"), sem("pick_ready"), sem("spread_ready")
        wdma, wtr, wcp, taps_ready = ([sem(f"{n}{l}") for l in range(2)] for n in ("wdma", "wtr", "wcp", "taps_ready"))

        class Norm:
            def __init__(self, n):
                self.loaded = [sem(f"{n}_loaded{r}") for r in range(RING)]
                self.stored = [sem(f"{n}_stored{r}") for r in range(RING)]
                self.copied = sem(f"{n}_copied")
                self.summed = sem(f"{n}_summed")
                self.centred = sem(f"{n}_centred")
                self.squared = sem(f"{n}_squared")
                self.var = sem(f"{n}_var")
                self.kept = sem(f"{n}_kept")
                self.std = sem(f"{n}_std")
                self.rstd = sem(f"{n}_rstd")
                self.spread = sem(f"{n}_spread")
                self.normed = sem(f"{n}_normed")
                self.mixed = sem(f"{n}_mixed")
                self.taken = sem(f"{n}_taken")
        ln = [Norm(f"ln{i}") for i in range(4)]
        state = [[sem(f"state{l}_{h}") for h in range(2)] for l in range(2)]
        conv = [[sem(f"conv{l}_{h}") for h in range(2)] for l in range(2)]

        relaid = [[sem(f"relaid{l}_{h}") for h in range(2)] for l in range(2)]
        top_max, top_found, exp_done, replaced, exp0_done, prob_diff, prob_ready = (
            sem(n) for n in ("top_max", "top_found", "exp_done", "replaced", "exp0_done", "prob_diff", "prob_ready"))
        prob_saved = sem("prob_saved")
        transposed, pool_mm, pool_read = sem("transposed"), sem("pool_mm"), sem("pool_read")
        tt_ready = [sem(f"tt_ready{j}") for j in range(2)]
        ew_dma, hid_mm, hid_act, eo_mm, outt_ready, lh_zero, lh_tr, lh_ready, lhg_ready = (
            sem(n) for n in ("ew_dma", "hid_mm", "hid_act", "eo_mm", "outt_ready", "lh_zero", "lh_tr", "lh_ready", "lhg_ready"))
        rdma, rnn_t, rnn_w_ready, bn_pe, bn_dve, bn_step, rnn_ready = (
            sem(n) for n in ("rdma", "rnn_t", "rnn_w_ready", "bn_pe", "bn_dve", "bn_step", "rnn_ready"))
        bn_std = sem("bn_std")
        pool_done = sem("pool_done")
        passed = sem("passed")
        step_mm, step_y, seg_done, x2_in, added, out_st = (
            sem(n) for n in ("step_mm", "step_y", "seg_done", "x2_in", "added", "out_st"))

        STEPS = [H - 1, H - 2, W - 1, W - 2]
        LINES0 = [1, H, 2 * H - 1, 2 * H + W - 2]
        STEPS0 = [0, H - 1, 2 * H - 3, 2 * H + W - 4]
        LINES = 2 * H + 2 * W - 4
        assert LINES == LINES0[3] + STEPS[3]

        def nat(t):
            v = t if len(t.shape) == 3 else t.rearrange("b c h w -> b c (h w)")
            return v.rearrange("(h b) c t -> h c b t", h=2)

        def nat_all(t):
            return t.rearrange("b c t -> c b t")

        def rows_view(p, h):
            return img[p[0]:p[1], h * HALF:(h + 1) * HALF].rearrange("p (b r j) -> p b r j", r=H, j=WP)

        def cols_view(p, h):
            return img[p[0]:p[1], h * HALF:(h + 1) * HALF].rearrange("p (b r j) -> p b r j", r=W, j=HP)

        LOW, HIGH, ALL = (0, 64), (64, 128), (0, 128)
        SIDE = (LOW, HIGH)

        def shape_of(k):
            rows = k < 2
            view, n, pairs = (rows_view, H, WP) if rows else (cols_view, W, HP)
            if k % 2 == 0:
                return view, int(rows), (lambda s: s), (lambda s: s + 1), pairs
            return view, int(rows), (lambda s: s * -1 + (n - 1)), (lambda s: s * -1 + (n - 2)), pairs

        SRC = [nat(x), nat(x), nat(t_dram), nat(x1_dram)]
        DST = [None, nat(t_dram), nat(x1_dram), nat(x2_dram)]
        EPS = [EPS_C, EPS_T, EPS_C, EPS_T]
        N2 = 2 * NCH
        PER = N2 // RING

        def unit(i, g, v):
            return 2 * g + v if i != 2 else g * -2 + (HB - 1 - v)

        def stat_rows(n):
            return n % 4, 2 * (n // 4)

        def token_pieces(k):
            a, b = k * CH, (k + 1) * CH
            if b <= SLOT:
                return [(0, 0, a, CH)]
            if a >= SLOT:
                return [(0, 1, a - SLOT, CH)]
            return [(0, 0, a, SLOT - a), (SLOT - a, 1, 0, b - SLOT)]

        def slot_tokens(z, b, a, m):
            return slots[:, z, ds(b, 1), a:a + m].rearrange("p b t -> p (b t)")

        def whole(b):
            return slots[:, :, ds(b, 1), :].rearrange("p z b t -> p z (b t)")

        spare = slots[:, :, HB, :]

        def own(eng):
            eng.sem_inc(passed, 1)

        NIT = S // (BODY * SEG)
        HIT = NIT // 2
        block = ctx.enter_context(nc.Block())

        def sp_norm(sp, i):
            st = ln[i]
            with sp.Fori(0, NG) as g:
                units = [sp.snap(unit(i, g, v)) for v in range(2)]

                def chunk(t, n):
                    v, k = n // NCH, n % NCH
                    return t[:, :, ds(units[v], 1), k * CH:(k + 1) * CH].rearrange("h c b t -> h c (b t)")

                def place(buf, n):
                    r = n % RING
                    return buf[:, r * CH:(r + 1) * CH]

                for n in range(RING):
                    sp.dma_start(place(ring, n), chunk(SRC[i], n)).then_inc(st.loaded[n % RING], 16)
                for n in range(N2):
                    if DST[i] is None:
                        sp.wait_ge(st.centred, g * N2 + (n + 1))
                        own(sp)
                    else:
                        sp.wait_ge(st.summed, g * N2 + (n + 1))
                        sp.dma_start(chunk(DST[i], n), place(sums, n)).then_inc(st.stored[n % RING], 16)
                    m = n + RING
                    if m < N2:
                        sp.dma_start(place(ring, m), chunk(SRC[i], m)).then_inc(st.loaded[m % RING], 16)
                if DST[i] is not None:
                    for r in range(RING):
                        sp.wait_ge(st.stored[r], 16 * (g * PER + PER))
                own(sp)

        def sp_taps(sp, l):
            for q in range(4):
                sp.dma_start(half(wraw, q % 2)[:, (q // 2) * C * KT:(q // 2 + 1) * C * KT],
                             conv_w[4 * l + q].rearrange("o i a b -> o (i a b)")).then_inc(wdma[l], 16)

        @block.sync
        def _(sp):
            sp.dma_start(graw[:, :], gate_w).then_inc(setup_dma, 16)
            for q in range(4):
                sp.dma_start(gbias[q * E:(q + 1) * E, :], gate_b.rearrange("(e a) -> e a", a=1)).then_inc(setup_dma, 16)
            sp_taps(sp, 0)
            sp.dma_start(wraw_r[:, 0:64], rnn_w).then_inc(rdma, 16)
            sp.dma_start(wraw_r[:, 64:128], rnn_v).then_inc(rdma, 16)
            sp.dma_start(gb[:, 0:1], gamma.rearrange("(e a) -> e a", a=1)).then_inc(rdma, 16)
            sp.dma_start(gb[:, 1:2], beta.rearrange("(e a) -> e a", a=1)).then_inc(rdma, 16)
            sp_norm(sp, 0)
            sp_norm(sp, 1)
            sp.wait_ge(pool_read, NG)
            sp.wait_ge(prob_saved, NG)
            for e0 in range(0, E, 7):
                n = min(7, E - e0)
                z, b = [(0, 1), (0, 3), (0, 5), (0, 7), (0, 8)][e0 // 7]
                sp.dma_start(slots[0:D1, z, b, 0:n * HID].rearrange("p (e h) -> p e h", e=n),
                             weight1[e0:e0 + n].rearrange("e d h -> d e h")).then_inc(ew_dma, 16)
            for c in range(2):
                for e0 in (0, 16):
                    sp.dma_start(slots[:, 1, 1 + 2 * (2 * c + e0 // 16), 0:16 * C].rearrange("p (e o) -> p e o", e=16),
                                 weight2[e0:e0 + 16, c * 128:(c + 1) * 128, :].rearrange("e p o -> p e o")).then_inc(ew_dma, 16)
            for e0 in (0, 16):
                sp.dma_start(b2_at(e0, 16).rearrange("p (e o) -> p e o", e=16),
                             weight2[e0:e0 + 16, HID:D2, :].rearrange("e p o -> p e o")).then_inc(ew_dma, 16)
            sp_taps(sp, 1)
            sp_norm(sp, 2)
            sp_norm(sp, 3)
            sp.wait_ge(rnn_ready, 1)
            with sp.Fori(0, NIT) as i:
                sp.dma_start(x2b, nat_all(x2_dram)[:, :, ds(i * (BODY * SEG), BODY * SEG)]).then_inc(x2_in, 16)
                sp.wait_ge(added, i * BODY + 2 * BODY)
                sp.dma_start(nat_all(out.rearrange("b c h w -> b c (h w)"))[:, :, ds(i * (BODY * SEG), BODY * SEG)],
                             ob).then_inc(out_st, 16)
            sp.wait_ge(out_st, 16 * (NIT + 1))

        @block.gpsimd
        def _(pool):
            done = [0]

            def alone(ins):
                done[0] += 1
                ins.then_inc(pool_done, 1)
                pool.wait_ge(pool_done, done[0])

            for buf, value in ((ident, 0.0), (average, 0.0), (fold, 0.0), (gate, 0.0), (wbd, 0.0), (taps, 0.0), (ones, 1.0),
                               (pooled, 1.0)):
                alone(pool.memset(buf[:, :], value))
            for n, value in enumerate(EPS + [EPS_BN]):
                alone(pool.memset(eps[:, n:n + 1], value))
            for h in range(2):
                alone(pool.memset(half(average, h)[:, h * 64:(h + 1) * 64], 1.0 / C))
            for base in (0, 64, -64):
                alone(pool.affine_select(out=fold[:, :], in_=fold[:, :], compare_op=ALU.not_equal, fill=0.5, base=base,
                                         pattern=[[-1, 128]], channel_multiplier=1))
            pool.affine_select(out=ident[:, :], in_=ident[:, :], compare_op=ALU.not_equal, fill=1.0, base=0,
                               pattern=[[-1, 128]], channel_multiplier=1).then_inc(consts, 1)
            alone(pool.memset(pick[:, :], 0.0))
            for h in range(2):
                alone(pool.memset(half(pick, h)[:, 126 + h:127 + h], 1.0 / C))
            alone(pool.memset(spread[:, :], 0.0))
            pool.sem_inc(pick_ready, 1)
            for n in range(N2 + 2):
                for h in range(2):
                    q, p = stat_rows(n)
                    part = spread[:, p * 64 + h * 64:p * 64 + (h + 1) * 64]
                    alone(pool.affine_select(out=part, in_=part, compare_op=ALU.not_equal, fill=1.0, base=-(32 * q + p + h),
                                             pattern=[[0, 64]], channel_multiplier=1))
            pool.sem_inc(spread_ready, 1)
            with pool.Fori(0, NG) as g:
                pool.wait_ge(prob_ready, g + 1)
                own(pool)
                pool.tensor_copy(whole(2 * g), spare).then_inc(prob_saved, 1)
            pool.wait_ge(eo_mm, 1)
            pool.memset(lh, 0.0).then_inc(lh_zero, 1)
            pool.wait_ge(lh_ready, 1)
            pool.tensor_copy(lhg[:, :], lh[:, (NG - 1) * 256:NG * 256]).then_inc(lhg_ready, 1)
            with pool.Fori(0, NG - 1) as g:
                pool.wait_ge(ln[2].summed, g * N2 + N2)
                own(pool)
                pool.tensor_copy(lhg[:, :], lh[:, ds(g * -256 + (NG - 2) * 256, 256)]).then_inc(lhg_ready, 1)

        def pe_taps(pe, l):
            pe.wait_ge(wdma[l], 64)
            wk = wraw.rearrange("p (a i k) -> p a k i", a=2, k=KT)
            for a in range(2):
                for k in range(KT):
                    if a == 1 and k % 4 == 0:
                        pe.wait_ge(wcp[l], k // 4 + 1)
                    last = pe.transpose(PS[4 + k // 4][0:64, (k % 4) * 128:(k % 4 + 1) * 128], wk[:, a, k, :], ident[:, :])
                    if k % 4 == 3 or k == KT - 1:
                        last.then_inc(wtr[l], 1)

        def pe_norm(pe, i, before=None, after=None, ending=None):
            st = ln[i]
            source = sums if DST[i] is not None else ring
            with pe.Fori(0, NG) as g:
                for n in range(N2 + 2):
                    if n < N2:
                        r = n % RING
                        if before:
                            before(g, n)
                        if i == 0:
                            pe.wait_ge(st.loaded[r], 16 * (g * PER + (n // RING + 1)))
                        else:
                            pe.wait_ge(st.summed, g * N2 + (n + 1))
                        if n >= RING:
                            pe.wait_ge(st.kept, g * N2 + (n - RING + 1))
                        pe.matmul(PS[r][:, 0:CH], centre[:, :], source[:, r * CH:(r + 1) * CH], start=True, stop=True
                                  ).then_inc(st.centred, 1)
                    if n >= 2:
                        m = n - 2
                        q, p = stat_rows(m)
                        c0 = 126 - 32 * q - p
                        pe.wait_ge(st.squared, g * N2 + (m + 1))
                        pe.matmul(PS[3][:, 0:CH], pick[:, c0:c0 + 128], sq[:, (m % 2) * CH:(m % 2 + 1) * CH],
                                  start=(m == 0), stop=(m == N2 - 1)).then_inc(st.var, 1)
                pe.wait_ge(st.rstd, g + 1)
                for n in range(N2 + 2):
                    if n < N2:
                        q, p = stat_rows(n)
                        if n >= RING:
                            pe.wait_ge(st.normed, g * N2 + (n - RING + 1))
                        pe.matmul(PS[n % RING][:, 0:CH], spread[32 * q:32 * q + 32, p * 64:p * 64 + 128],
                                  rstd[32 * q:32 * q + 32, :], start=True, stop=True).then_inc(st.spread, 1)
                    if n >= 2 and after:
                        after(g, n - 2)
                pe.wait_ge(st.normed, g * N2 + N2)
                if ending:
                    ending(g)
                own(pe)

        def pe_sweep(pe, l, k):
            view, s0, src, _, pairs = shape_of(k)
            with pe.Fori(0, STEPS[k]) as s:
                at = pe.snap(src(s))
                for h in range(2):
                    acc = PS[h][:, 0:HB * pairs].rearrange("p (b j) -> p b j", b=HB)
                    v = view(ALL, h)
                    pe.wait_ge(state[l][h], s + LINES0[k])
                    for n, d in enumerate(OFFS):
                        lo, hi = max(0, -d), min(pairs, pairs - d)
                        last = pe.matmul(acc[:, :, lo:hi], taps[:, (k * NO + d + 2) * 128:(k * NO + d + 3) * 128],
                                         v[:, s0:s0 + HB, ds(at, 1), lo + d:hi + d].rearrange("p b r j -> p b (r j)"),
                                         start=(n == 0), stop=(n == NO - 1))
                    last.then_inc(conv[l][h], 1)

        def logits(pe, g, n):
            if n < NCH:
                return
            k = n - NCH
            if k >= 2:
                pe.wait_ge(ln[1].taken, g * NCH + (k - 1))
            pe.wait_ge(ln[1].normed, g * N2 + (n + 1))
            for v in range(2):
                last = pe.matmul(PS[5 + k % 2][:, 0:CH], gate[:, v * 128:(v + 1) * 128],
                                 xl[:, v * S + k * CH:v * S + (k + 1) * CH], start=(v == 0), stop=(v == 1))
            last.then_inc(ln[1].mixed, 1)

        def pooling(pe, g):
            pe.wait_ge(prob_ready, g + 1)
            for c in range(NTC + 1):
                if c < NTC:
                    bank = PS[5 + c % 2]
                    if c >= 2:
                        pe.wait_ge(tt_ready[c % 2], g * (NTC // 2) + c // 2)
                    pe.transpose(bank[0:TC, 0:128], slots[:, c // (NTC // 2), HB, (c % (NTC // 2)) * TC:(c % (NTC // 2) + 1) * TC], ident[:, :])
                    for v in range(2):
                        last = pe.transpose(bank[0:TC, 128 + v * 128:256 + v * 128],
                                            xl[:, v * S + c * TC:v * S + (c + 1) * TC], ident[:, :])
                    last.then_inc(transposed, 1)
                if c >= 1:
                    m = c - 1
                    pe.wait_ge(tt_ready[m % 2], g * (NTC // 2) + (m // 2 + 1))
                    o = (m % 2) * 384
                    for v in range(2):
                        last = pe.matmul(PS[v][:, 0:64], tt[:, o + 128 + v * 128:o + 256 + v * 128],
                                         tt[:, o + v * 64:o + (v + 1) * 64], start=(m == 0), stop=(m == NTC - 1))
                    last.then_inc(pool_mm, 1)
            pe.wait_ge(pool_read, g + 1)

        def mixture(pe, g, n):
            v, k = n // NCH, n % NCH
            if n == 0:
                pe.wait_ge(lhg_ready, g + 1)
            if n >= 2:
                pe.wait_ge(ln[2].summed, g * N2 + (n - 1))
            for o, z, a, m in token_pieces(k):
                last = pe.matmul(PS[5 + n % 2][:, o:o + m], lhg[:, (1 - v) * 128:(2 - v) * 128],
                                 slot_tokens(z, (HB - 2) - 2 * g, a, m), start=True, stop=True)
            last.then_inc(ln[2].mixed, 1)

        def rnn_input(pe, g, n):
            v, k = n // NCH, n % NCH
            if n >= 2:
                pe.wait_ge(ln[3].taken, g * N2 + (n - 1))
            pe.wait_ge(ln[3].normed, g * N2 + (n + 1))
            for o, z, a, m in token_pieces(k):
                last = pe.matmul(PS[5 + n % 2][:, o:o + m], wbd[:, :], slot_tokens(z, 2 * g + v, a, m), start=True, stop=True)
            last.then_inc(ln[3].mixed, 1)

        def fill_input(pe, bank, h, z, t0, c0, w, first):
            acc = PS[bank][0:64, 0:SEG * B].rearrange("p (t b) -> p b t", b=B)
            tok = slots[:, ds(z, 1), 0:HB, ds(t0 + c0, w)].rearrange("p z b t -> p (z b) t")
            pe.matmul(acc[:, h * HB:(h + 1) * HB, c0:c0 + w], wsc[h], tok, start=first, stop=True, skip_group_check=True)

        @block.tensor
        def _(pe):
            pe.wait_ge(consts, 1)
            pe.wait_ge(setup_dma, 80)
            pe.transpose(PS[7][0:C, 0:E], graw[:, :], ident[0:E, 0:E]).then_inc(gate_t, 1)
            pe.wait_ge(rdma, 64)
            pe.wait_ge(gate_ready, 1)
            for a in range(2):
                last = pe.transpose(PS[7][0:64, 64 + a * 64:128 + a * 64], wraw_r[:, a * 64:(a + 1) * 64], ident[0:64, 0:64])
            last.then_inc(rnn_t, 1)
            pe_taps(pe, 0)
            pe.wait_ge(wcp[0], 6)
            pe.wait_ge(centre_ready, 1)
            pe.wait_ge(pick_ready, 1)
            pe.wait_ge(spread_ready, 1)
            pe_norm(pe, 0)
            pe.wait_ge(taps_ready[0], 1)
            for k in range(4):
                pe_sweep(pe, 0, k)
            pe.wait_ge(gate_ready, 1)
            pe_norm(pe, 1, after=lambda g, n: logits(pe, g, n), ending=lambda g: pooling(pe, g))

            pe.wait_ge(ew_dma, 16 * 11)
            pv = pooled[:, :].rearrange("p (b e) -> p e b", e=E)
            for e in range(E):
                for c in range(2):
                    last = pe.matmul(PS[e // 16][:, (e % 16) * 32 + c * 16:(e % 16) * 32 + (c + 1) * 16],
                                     w1_at(e)[:, c * 128:(c + 1) * 128], pv[:, e, :], start=True, stop=True)
                if e % 16 == 15:
                    last.then_inc(hid_mm, 1)
            eo = PS[2][0:64, :].rearrange("p (b e) -> p e b", e=E)
            for e in range(E):
                if e % 16 == 0:
                    pe.wait_ge(hid_act, e // 16 + 1)
                for c in range(2):
                    pe.matmul(eo[:, e, :], w2_at(c, e), hidden[:, e * 32 + c * 16:e * 32 + (c + 1) * 16],
                              start=(c == 0), stop=False)
                last = pe.matmul(eo[:, e, :], b2_at(e), ones[:, 0:B], start=False, stop=True)
            last.then_inc(eo_mm, 1)
            pe.wait_ge(outt_ready, 1)
            for g in range(NG):
                last = pe.transpose(PS[3][:, g * 64:(g + 1) * 64], outt[:, g * 128:(g + 1) * 128], ident[0:64, 0:64])
            last.then_inc(lh_tr, 1)
            pe_taps(pe, 1)
            pe.wait_ge(wcp[1], 6)
            pe_norm(pe, 2, before=lambda g, n: mixture(pe, g, n))
            pe.wait_ge(taps_ready[1], 1)
            for k in range(4):
                pe_sweep(pe, 1, k)
            pe.wait_ge(rnn_w_ready, 1)
            pe_norm(pe, 3, after=lambda g, n: rnn_input(pe, g, n))

            pe.wait_ge(bn_dve, 1)
            pe.matmul(PS[7][:, 0:1], fold[:, :], bnm[:, 0:1], start=True, stop=True).then_inc(bn_pe, 1)
            pe.wait_ge(bn_dve, 2)
            pe.matmul(PS[7][:, 2:3], fold[:, :], bnm[:, 3:4], start=True, stop=True).then_inc(bn_pe, 1)
            pe.wait_ge(bn_dve, 3)
            pe.transpose(PS[7][0:64, 64:128], wrow, ident[0:64, 0:64])
            pe.transpose(PS[7][0:1, 128:192], bnm[0:64, 8:9], ident[0:64, 0:64]).then_inc(bn_pe, 1)
            pe.wait_ge(rnn_ready, 1)

            with pe.Fori(0, 2) as z:
                with pe.Fori(0, HIT) as j:
                    t0 = j * (BODY * SEG)
                    for h in range(2):
                        fill_input(pe, 0, h, z, t0, 0, SEG, h == 0)
                    for s in range(BODY):
                        for t in range(SEG):
                            n = s * SEG + t
                            if n == 0:
                                pe.wait_ge(step_y, BODY * SEG)
                                pe.sem_clear(step_y)
                            else:
                                pe.wait_ge(step_y, n)
                            if t == 0:
                                pe.sem_inc(seg_done, 1)
                            prev = yb[:, s, :, t - 1] if t else yb[:, (s - 1) % BODY, :, SEG - 1]
                            for c in range(2):
                                last = pe.matmul(PS[s % 2][c * 32:(c + 1) * 32, t * B:(t + 1) * B], vt[:, c * 32:(c + 1) * 32],
                                                 prev, start=False, stop=True, skip_group_check=True)
                            last.then_inc(step_mm, 1)
                            if s < BODY - 1 and t < 20:
                                fill_input(pe, (s + 1) % 2, t // 10, z, t0 + (s + 1) * SEG, (t % 10) * 3, 3, t == 0)
            pe.wait_ge(step_y, BODY * SEG)
            pe.sem_inc(seg_done, 1)

        def act_relayout(act, l):
            relayout(act, l, 1, lambda o, a: act.activation(o, a, ACT.Copy))

        def relayout(eng, l, h, move):
            eng.wait_ge(state[l][h], LINES0[2] - 1)
            eng.sem_inc(relaid[l][h], 1)
            with eng.Fori(0, HB) as b:
                eng.wait_ge(relaid[l][h], b + 1)
                own(eng)
                for hp in range(2):
                    for wp in range(2):
                        dst = cols_view(SIDE[hp], h)[:, ds(b, 1), wp::2, :].rearrange("p b w j -> p (b w) j")
                        src = rows_view(SIDE[wp], h)[:, ds(b + 1, 1), hp::2, :].rearrange("p b r j -> p j (b r)")
                        last = move(dst, src)
                last.then_inc(relaid[l][h], 1)
            eng.wait_ge(relaid[l][h], HB + 1)
            eng.sem_inc(state[l][h], 1)

        def act_norm(act, i, copy=False, ending=None):
            st = ln[i]
            with act.Fori(0, NG) as g:
                def natural(v, piece):
                    h, hp = piece // 2, piece % 2
                    dst = half(xl, h)[:, v * S:(v + 1) * S].rearrange("p (r w) -> p r w", w=W)[:, hp::2, :]
                    src = cols_view(SIDE[hp], h)[:, ds(unit(i, g, v), 1), :, :].rearrange("p b w j -> p j (b w)")
                    ins = act.activation(dst, src, ACT.Copy)
                    if piece == 3:
                        ins.then_inc(st.copied, 1)
                if copy:
                    for piece in range(4):
                        natural(0, piece)
                for n in range(N2):
                    act.wait_ge(st.kept, g * N2 + (n + 1))
                    if n >= 2:
                        act.wait_ge(st.var, g * N2 + (n - 1))
                    act.activation(sq[:, (n % 2) * CH:(n % 2 + 1) * CH], xl[:, n * CH:(n + 1) * CH], ACT.Square
                                   ).then_inc(st.squared, 1)
                    if copy and n in (1, 3, 5, 7):
                        natural(1, n // 2)
                act.wait_ge(st.var, g * N2 + N2)
                act.activation(rstd[:, :], PS[3][:, 0:CH], ACT.Sqrt, bias=eps[:, i:i + 1]).then_inc(st.std, 1)
                if ending:
                    ending(g)
                elif copy:
                    act.wait_ge(st.normed, g * N2 + N2)
                    own(act)

        def take_logits(act, g, k):
            act.wait_ge(ln[1].mixed, g * NCH + (k + 1))
            for o, z, a, m in token_pieces(k):
                last = act.activation(spare[:, z, a:a + m], PS[5 + k % 2][:, o:o + m], ACT.Identity, bias=gbias[:, 0:1])
            last.then_inc(ln[1].taken, 1)

        def route(act, g):
            for k in range(NCH):
                take_logits(act, g, k)
            act.wait_ge(top_found, g + 1)
            own(act)
            act.activation(whole(2 * g), spare, ACT.Exp, bias=stat[:, 0:1], accum_out=stat[:, 1:2]).then_inc(exp_done, 1)
            act.wait_ge(replaced, g + 1)
            act.activation(spare, spare, ACT.Exp, bias=stat[:, 0:1]).then_inc(exp0_done, 1)
            sums_stored(act, g)
            for c in range(1, NTC, 2):
                take_transposed(act, g, c, lambda o, a: act.activation(o, a, ACT.Copy))
            act.wait_ge(pool_mm, g * NTC + NTC)
            for v in range(2):
                for h in range(2):
                    last = act.activation(pooled[0:C, ds(g * 128 + (2 * v + h) * E, E)],
                                          half(PS[v], h)[:, h * E:(h + 1) * E], ACT.Copy)
            last.then_inc(pool_read, 1)
            act.wait_ge(prob_saved, g + 1)
            own(act)

        def sums_stored(eng, g):
            for r in range(RING):
                eng.wait_ge(ln[1].stored[r], 16 * (g * PER + PER))
            own(eng)

        def take_transposed(eng, g, c, move):
            eng.wait_ge(transposed, g * NTC + (c + 1))
            if c >= 2:
                eng.wait_ge(pool_mm, g * NTC + (c - 1))
            move(tt[:, (c % 2) * 384:(c % 2 + 1) * 384], PS[5 + c % 2][0:TC, 0:384]).then_inc(tt_ready[c % 2], 1)

        @block.scalar
        def _(act):
            act.wait_ge(setup_dma, 80)
            act.wait_ge(consts, 1)
            act_norm(act, 0)
            act_relayout(act, 0)
            for h in range(2):
                act.wait_ge(state[0][h], LINES)
            act_norm(act, 1, copy=True, ending=lambda g: route(act, g))
            for j in range(2):
                act.wait_ge(hid_mm, j + 1)
                act.activation(hidden[:, j * 512:(j + 1) * 512], PS[j][:, :], ACT.Gelu).then_inc(hid_act, 1)
            act_norm(act, 2)
            act_relayout(act, 1)
            for h in range(2):
                act.wait_ge(state[1][h], LINES)
            act_norm(act, 3, copy=True)
            act.wait_ge(bn_pe, 2)
            act.activation(bnm[0:64, 4:5], PS[7][0:64, 2:3], ACT.Sqrt, bias=eps[0:64, 4:5]).then_inc(bn_std, 1)
            act.wait_ge(rnn_ready, 1)
            act.activation(warm[:, :], ones[0:1, 0:1], ACT.Sigmoid)
            with act.Fori(0, NIT) as i:
                for s in range(BODY):
                    act.wait_ge(added, i * BODY + (s + 1))
                    for t in range(SEG):
                        n = s * SEG + t
                        act.wait_ge(step_mm, n + 1)
                        if n == BODY * SEG - 1:
                            act.sem_clear(step_mm)
                        act.activation(yb[0:64, s, :, t], PS[s % 2][0:64, t * B:(t + 1) * B], ACT.Sigmoid).then_inc(step_y, 1)

        def dve_taps(dve, l):
            for a in range(2):
                for j, (k0, k1) in enumerate(((0, 4), (4, 8), (8, 9))):
                    dve.wait_ge(wtr[l], a * 3 + j + 1)
                    dve.tensor_copy(wt[:, a, k0:k1, :, :],
                                    PS[4 + j][0:64, 0:(k1 - k0) * 128].rearrange("p (k s o) -> p k s o", s=2, o=64)
                                    ).then_inc(wcp[l], 1)

            dve.wait_ge(wcp[l], 6)
            for q in range(4):
                for ip in range(2):
                    for op in range(2):
                        d0, d1 = (-2, 2) if ip == op else (-1, 2) if ip < op else (-2, 1)
                        k0 = 2 * d0 + 4 + ip - op
                        dst = half(taps, ip)[:, q * NO * 128:(q + 1) * NO * 128].rearrange("p (d o c) -> p d o c", d=NO, o=2)
                        last = dve.tensor_copy(dst[:, d0 + 2:d1 + 3, op, :], wt[:, q // 2, k0:k0 + 2 * (d1 - d0) + 1:2, q % 2, :])
            last.then_inc(taps_ready[l], 1)
            dve.wait_ge(taps_ready[l], 1)

        def dve_norm(dve, i, later=None, ending=None):
            st = ln[i]
            with dve.Fori(0, NG) as g:
                units = [dve.snap(unit(i, g, v) + 1) for v in range(2)]
                for n in range(N2 + 1):
                    if n < N2 and i > 0:
                        v, k, r = n // NCH, n % NCH, n % RING
                        rc = ring[:, r * CH:(r + 1) * CH]
                        dve.wait_ge(st.loaded[r], 16 * (g * PER + (n // RING + 1)))
                        if n >= RING:
                            dve.wait_ge(st.stored[r], 16 * (g * PER + n // RING))
                        if i == 2:
                            dve.wait_ge(st.mixed, g * N2 + (n + 1))
                            add = PS[5 + n % 2][:, 0:CH]
                        else:
                            dve.wait_ge(st.copied, g * 2 + (v + 1))
                            add = xl[:, v * S + k * CH:v * S + (k + 1) * CH]
                        dve.tensor_tensor(sums[:, r * CH:(r + 1) * CH], add, rc, ALU.add).then_inc(st.summed, 1)
                    if n >= 1:
                        m = n - 1
                        dve.wait_ge(st.centred, g * N2 + (m + 1))
                        dve.tensor_copy(xl[:, m * CH:(m + 1) * CH], PS[m % RING][:, 0:CH]).then_inc(st.kept, 1)
                dve.wait_ge(st.std, g + 1)
                dve.reciprocal(rstd[:, :], rstd[:, :]).then_inc(st.rstd, 1)
                for n in range(N2 + 2):
                    if n < N2:
                        v, k = n // NCH, n % NCH
                        xc, rs = xl[:, n * CH:(n + 1) * CH], PS[n % RING][:, 0:CH]
                        dve.wait_ge(st.spread, g * N2 + (n + 1))
                        if i in (0, 2):
                            for h in range(2):
                                for wp in range(2):
                                    dst = rows_view(SIDE[wp], h)[:, ds(units[v], 1), k * CH_ROWS:(k + 1) * CH_ROWS, :]
                                    parity = (lambda t: half(t, h).rearrange("p (r j e) -> p r j e", j=WP, e=2)[:, :, :, wp])
                                    last = dve.tensor_tensor(dst.rearrange("p b r j -> p (b r) j"), parity(xc), parity(rs), ALU.mult)
                        elif i == 1:
                            last = dve.tensor_tensor(xc, xc, rs, ALU.mult)
                        else:
                            for o, z, a, c in token_pieces(k):
                                last = dve.tensor_tensor(slot_tokens(z, 2 * g + v, a, c), xc[:, o:o + c], rs[:, o:o + c], ALU.mult)
                        last.then_inc(st.normed, 1)
                    if n >= 2 and later:
                        later(g, n - 2)
                if ending:
                    ending(g)

        def dve_route(dve, g):
            dve.wait_ge(ln[1].taken, g * NCH + NCH)
            own(dve)
            dve.max(top8[:, :], spare).then_inc(top_max, 1)
            dve.wait_ge(top_max, g + 1)
            dve.tensor_scalar(stat[:, 0:1], top8[:, 0:1], -1.0, None, ALU.mult).then_inc(top_found, 1)
            dve.wait_ge(exp_done, g + 1)
            own(dve)
            dve.match_replace(spare, top8[:, :], spare, -1e30).then_inc(replaced, 1)
            dve.reciprocal(stat[:, 2:3], stat[:, 1:2])
            dve.wait_ge(exp0_done, g + 1)
            dve.tensor_tensor(spare, whole(2 * g), spare, ALU.subtract).then_inc(prob_diff, 1)
            dve.wait_ge(prob_diff, g + 1)
            dve.tensor_scalar(spare, spare, stat[:, 2:3], None, ALU.mult).then_inc(prob_ready, 1)
            sums_stored(dve, g)
            for c in range(0, NTC, 2):
                take_transposed(dve, g, c, lambda o, a: dve.tensor_copy(o, a))

        def dve_sweep(dve, l, k):
            view, s0, _, target, pairs = shape_of(k)
            with dve.Fori(0, STEPS[k]) as s:
                at = dve.snap(target(s))
                for h in range(2):
                    acc = PS[h][:, 0:HB * pairs].rearrange("p (b j) -> p b j", b=HB)
                    line = view(ALL, h)[:, s0:s0 + HB, ds(at, 1), :].rearrange("p b r j -> p b (r j)")
                    dve.wait_ge(conv[l][h], s + (STEPS0[k] + 1))
                    dve.scalar_tensor_tensor(out=line, in0=acc, scalar=0.0, in1=line, op0=ALU.max, op1=ALU.add
                                             ).then_inc(state[l][h], 1)

        def dve_layer(dve, l):
            dve.wait_ge(ln[2 * l].normed, NG * N2)
            for h in range(2):
                dve.sem_inc(state[l][h], 1)
            dve_sweep(dve, l, 0)
            dve_sweep(dve, l, 1)
            relayout(dve, l, 0, lambda o, a: dve.tensor_copy(o, a))
            dve_sweep(dve, l, 2)
            dve_sweep(dve, l, 3)

        def bn_take(dve, g, n):
            dve.wait_ge(ln[3].mixed, g * N2 + (n + 1))
            dve.bn_stats(bns[:, ds(g * (N2 * 6) + n * 6, 6)], PS[5 + n % 2][:, 0:CH]).then_inc(ln[3].taken, 1)

        @block.vector
        def _(dve):
            dve.wait_ge(consts, 1)
            dve.tensor_tensor(centre[:, :], ident[:, :], average[:, :], ALU.subtract).then_inc(centre_ready, 1)
            dve.wait_ge(gate_t, 1)
            for v in range(2):
                for h in range(2):
                    c0 = v * 128 + v * 64 + h * E
                    last = dve.tensor_copy(half(gate, h)[:, c0:c0 + E], PS[7][0:C, 0:E])
            last.then_inc(gate_ready, 1)
            dve.wait_ge(rnn_t, 1)
            for h in range(2):
                dve.tensor_copy(half(wbd, h)[:, h * 64:(h + 1) * 64], PS[7][0:64, 64:128])
            dve.tensor_copy(vt[0:64, :], PS[7][0:64, 128:192]).then_inc(rnn_w_ready, 1)
            dve_taps(dve, 0)
            dve_norm(dve, 0)
            dve_layer(dve, 0)
            dve_norm(dve, 1, ending=lambda g: dve_route(dve, g))
            dve.wait_ge(eo_mm, 1)
            dve.tensor_copy(outt, PS[2][0:64, :]).then_inc(outt_ready, 1)
            dve.wait_ge(lh_zero, 1)
            dve.wait_ge(lh_tr, 1)
            for g in range(NG):
                for v in range(2):
                    for h in range(2):
                        p, c0 = v * 64 + h * E, (2 * g + v) * 128 + h * 64
                        last = dve.tensor_copy(lh[p:p + E, c0:c0 + 64], PS[3][p:p + E, g * 64:(g + 1) * 64])
            last.then_inc(lh_ready, 1)
            dve_taps(dve, 1)
            dve_norm(dve, 2)
            dve_layer(dve, 1)
            dve_norm(dve, 3, later=lambda g, n: bn_take(dve, g, n))

            def link(ins, n):
                ins.then_inc(bn_step, 1)
                dve.wait_ge(bn_step, n)
            dve.wait_ge(ln[3].taken, NG * N2)
            dve.bn_aggr(bnm[:, 0:2], bns[:, :]).then_inc(bn_dve, 1)
            dve.wait_ge(bn_pe, 1)
            link(dve.tensor_tensor(bnm[:, 2:3], bnm[:, 0:1], PS[7][:, 0:1], ALU.subtract), 1)
            dve.scalar_tensor_tensor(out=bnm[:, 3:4], in0=bnm[:, 2:3], scalar=bnm[:, 2:3], in1=bnm[:, 1:2],
                                     op0=ALU.mult, op1=ALU.add).then_inc(bn_dve, 1)
            dve.wait_ge(bn_std, 1)
            link(dve.reciprocal(bnm[0:64, 5:6], bnm[0:64, 4:5]), 2)
            link(dve.tensor_tensor(bnm[0:64, 6:7], bnm[0:64, 5:6], gb[:, 0:1], ALU.mult), 3)
            link(dve.tensor_tensor(bnm[0:64, 7:8], PS[7][0:64, 0:1], bnm[0:64, 6:7], ALU.mult), 4)
            link(dve.tensor_tensor(bnm[0:64, 8:9], gb[:, 1:2], bnm[0:64, 7:8], ALU.subtract), 5)
            dve.tensor_scalar(wrow, wraw_r[:, 0:64], bnm[0:64, 6:7], None, ALU.mult).then_inc(bn_dve, 1)
            for h in range(2):
                link(dve.memset(wsc[h], 0.0), 6 + h)
            link(dve.memset(yb[64:65], 1.0), 8)
            dve.memset(yb[0:64, BODY - 1, :, SEG - 1], 0.0).then_inc(step_y, BODY * SEG)
            dve.wait_ge(bn_pe, 3)
            for h in range(2):
                dve.tensor_copy(half(wsc[h], h), PS[7][0:64, 64:128])
            dve.tensor_copy(vt[64:65, :], PS[7][0:1, 128:192]).then_inc(rnn_ready, 1)
            dve.sem_inc(added, BODY)
            dve.sem_inc(out_st, 16)
            with dve.Fori(0, NIT) as i:
                dve.wait_ge(x2_in, i * 16 + 16)
                dve.wait_ge(out_st, i * 16 + 16)
                for s in range(BODY):
                    dve.wait_ge(seg_done, i * BODY + (s + 2))
                    dve.tensor_tensor(ob[:, :, s * SEG:(s + 1) * SEG], x2b[:, :, s * SEG:(s + 1) * SEG], yb[0:64, s, :, :],
                                      ALU.add).then_inc(added, 1)


_INS = ['x', 'L0_conv_w_d', 'L0_conv_w_u', 'L0_conv_w_r', 'L0_conv_w_l', 'L0_ffn_gate_w', 'L0_ffn_gate_b', 'L0_ffn_weight1',
        'L0_ffn_weight2', 'L1_conv_w_d', 'L1_conv_w_u', 'L1_conv_w_r', 'L1_conv_w_l', 'L1_ffn_W', 'L1_ffn_V', 'L1_ffn_gamma',
        'L1_ffn_beta']
_OUTS = [((B, C, H, W), 'float32')]


def kernel(**inputs):
    import numpy as _np
    import concourse.bacc as _bacc
    from concourse import mybir as _mybir
    from concourse.bass_utils import run_bass_kernel_spmd as _run

    nc = _bacc.Bacc("TRN2", target_bir_lowering=False, num_devices=1)
    arrays, a = {}, {}
    for name in _INS:
        v = _np.ascontiguousarray(inputs[name])
        arrays[f"in_{name}_dram"] = v
        a[name] = nc.dram_tensor(f"in_{name}_dram", v.shape, _mybir.dt.from_np(v.dtype), kind="ExternalInput").ap()
    outs = [nc.dram_tensor(f"out_{i}_dram", shape, _mybir.dt.from_np(_np.dtype(dtype)), kind="ExternalOutput").ap()
            for i, (shape, dtype) in enumerate(_OUTS)]
    scratch = [nc.dram_tensor(f"{n}_dram", (B, C, S), _mybir.dt.float32, kind="Internal").ap() for n in ("t", "x1", "x2")]
    metaformer(nc, a['x'], [a[f"L{l}_conv_w_{d}"] for l in range(2) for d in "durl"], a['L0_ffn_gate_w'], a['L0_ffn_gate_b'],
               a['L0_ffn_weight1'], a['L0_ffn_weight2'], a['L1_ffn_W'], a['L1_ffn_V'], a['L1_ffn_gamma'], a['L1_ffn_beta'],
               outs[0], *scratch)
    r = _run(nc, [arrays], core_ids=[0])
    return r.results[0]["out_0_dram"]
```

```python
import concourse.bass as bass
from concourse import mybir
from contextlib import ExitStack

B, C, H, W = 16, 64, 36, 100
HB = B // 2
S = H * W
HP, WP = H // 2, W // 2
SLOT = S // 2
HALF = (HB + 1) * SLOT
KT = 9
OFFS = (0, -2, -1, 1, 2)
NO = len(OFFS)
CH_ROWS = 4
CH = CH_ROWS * W
NCH = H // CH_ROWS
RING = 3
E, D1, HID, D2, TOPK = 32, C + 1, 256, 257, 8
NG = 4
TC = 120
NTC = S // TC
EDGE = 2
SPLIT_TAPS = 2 * 2 * NO * 128
SPLIT_LINES = 4 * HB * (WP + 2 * EDGE)
SEG = 30
BODY = 4
EPS_C, EPS_T, EPS_BN = 1e-6, 1e-5, 1e-5
GONE = -3e38


def metaformer(nc, x, conv_w, gate_w, gate_b, weight1, weight2, rnn_w, rnn_v, gamma, beta, out, t_dram, x1_dram, x2_dram):
    fp32, fp32r = mybir.dt.float32, mybir.dt.float32r
    ALU = mybir.AluOpType
    ACT = mybir.ActivationFunctionType
    ds = bass.ds

    with ExitStack() as ctx:
        def sb(name, shape):
            return ctx.enter_context(nc.sbuf_tensor(name, shape, fp32))

        def sem(name):
            return ctx.enter_context(nc.semaphore(name))

        img = sb("img", [128, 2 * HALF])
        with nc.sbuf_tensor("split", [128, SPLIT_TAPS + SPLIT_LINES], fp32r) as split:
            pass
        xl = sb("xl", [128, 2 * S])
        ring = sb("ring", [128, RING * CH])
        sq = sb("sq", [128, 2 * CH])
        sums = sb("sums", [128, RING * CH])
        rparts = ctx.enter_context(nc.sbuf_tensor("rparts", [128, 2 * CH], fp32r))
        rstd = sb("rstd", [128, CH])
        pick = sb("pick", [128, 254])
        spread = ctx.enter_context(nc.sbuf_tensor("spread", [128, 5 * 128], fp32r))
        taps = sb("taps", [128, 4 * NO * 128])
        tt = sums[0:TC, 0:RING * 384]
        tt_pool = sq[:, 0:128]
        pooled_bns = sb("pooled_bns", [128, B * E])
        pooled = pooled_bns[0:D1, :]
        bns = pooled_bns[:, 0:NG * 2 * NCH * 6]
        ident = sb("ident", [128, 128])
        centre = sb("centre", [128, 128])
        average = sq[:, 0:128]
        gate_lhg = sb("gate_lhg", [128, 2 * 128])
        gate = gate_lhg[:, :]
        gbias = sb("gbias", [128, 1])
        top8 = sb("top8", [128, TOPK])
        stat = sb("stat", [128, 8])
        lhg = gate_lhg[:, :]
        graw = sb("graw", [E, C])
        vt = sb("vt", [65, 64])
        wraw_r = sb("wraw_r", [64, 128])
        wbd = sb("wbd", [128, 128])
        gb = sb("gb", [64, 2])
        bnm = sb("bnm", [128, 16])
        fold = sb("fold", [128, 128])
        warm = sb("warm", [1, 1])
        eps = sb("eps", [128, 5])
        ones = sb("ones", [1, B])
        PS = [ctx.enter_context(nc.psum_tensor(f"ps{i}", [128, 512], fp32)) for i in range(8)]

        def half(buf, h):
            return buf[h * 64:(h + 1) * 64]

        wraw = xl[:, 0:2 * C * KT]
        wt = xl[0:64, 2 * C * KT:2 * C * KT + 2 * KT * 128].rearrange("p (a k s o) -> p a k s o", a=2, k=KT, s=2)
        hidden = xl[:, S + 1024:S + 2048]
        outt = xl[0:64, S + 2048:S + 2560]
        yb = xl[0:65, 0:BODY * SEG * B].rearrange("p (s b t) -> p s b t", s=BODY, b=B)
        x2b = xl[0:64, 1920:3840].rearrange("p (b t) -> p b t", b=B)
        ob = xl[0:64, 3840:5760].rearrange("p (b t) -> p b t", b=B)
        wsc = [xl[:, 5760 + h * 64:5824 + h * 64] for h in range(2)]
        wrow = xl[0:64, 5888:5952]
        taps_part = [split[:, p * 2 * NO * 128:(p + 1) * 2 * NO * 128] for p in range(2)]

        def split_line(h, part):
            n = HB * (WP + 2 * EDGE)
            a = SPLIT_TAPS + (2 * h + part) * n
            return split[:, a:a + n].rearrange("p (b j) -> p b j", b=HB)

        def line_pairs(h, part, d=0):
            return split_line(h, part)[:, :, EDGE + d:EDGE + d + WP]

        slots = img[:, :].rearrange("p (z b t) -> p z b t", z=2, b=HB + 1)

        lh = slots[:, 0, 1, 0:2 * NG * 128]

        def w1_at(e):
            if e < 28:
                return slots[0:D1, 0, 1 + 2 * (e // 7), (e % 7) * HID:(e % 7 + 1) * HID]
            b, a = (3, e - 28) if e < 31 else (5, 0)
            return slots[0:D1, 1, b, 16 * C + a * HID:16 * C + (a + 1) * HID]

        def w2_at(c, e):
            return slots[:, 1, 1 + 2 * (2 * c + e // 16), (e % 16) * C:(e % 16 + 1) * C]

        def b2_at(e, n=1):
            if e % 16 < 12:
                b, a = (7, 1)[e // 16], 16 * C + (e % 16) * C
            else:
                b, a = 5, 16 * C + HID + (e // 16) * 4 * C + (e % 16 - 12) * C
            return slots[0:1, 1, b, a:a + n * C]

        setup_dma, consts, gate_t, gate_ready = sem("setup_dma"), sem("consts"), sem("gate_t"), sem("gate_ready")
        centre_ready, pick_ready, spread_ready = sem("centre_ready"), sem("pick_ready"), sem("spread_ready")
        wdma, wtr, wcp, taps_ready = ([sem(f"{n}{l}") for l in range(2)] for n in ("wdma", "wtr", "wcp", "taps_ready"))

        class Norm:
            def __init__(self, n):
                self.loaded = [sem(f"ln{n}_loaded{r}") for r in range(RING)]
                if n > 0:
                    self.stored = [sem(f"ln{n}_stored{r}") for r in range(RING)]
                    self.summed = sem(f"ln{n}_summed")
                    self.mixed = sem(f"ln{n}_mixed")
                if n in (1, 3):
                    self.copied = sem(f"ln{n}_copied")
                    self.taken = sem(f"ln{n}_taken")
                self.centred = sem(f"ln{n}_centred")
                self.squared = sem(f"ln{n}_squared")
                self.var = sem(f"ln{n}_var")
                self.kept = sem(f"ln{n}_kept")
                self.std = sem(f"ln{n}_std")
                self.inverse = sem(f"ln{n}_inverse")
                self.high = sem(f"ln{n}_high")
                self.rstd = sem(f"ln{n}_rstd")
                self.spread = sem(f"ln{n}_spread")
                self.normed = sem(f"ln{n}_normed")
        ln = [Norm(i) for i in range(4)]
        state = [[sem(f"state{l}_{h}") for h in range(2)] for l in range(2)]
        hi = [[sem(f"hi{l}_{h}") for h in range(2)] for l in range(2)]
        lo = [[sem(f"lo{l}_{h}") for h in range(2)] for l in range(2)]
        taps_hi, taps_lo = ([sem(f"{n}{l}") for l in range(2)] for n in ("taps_hi", "taps_lo"))
        conv = [[sem(f"conv{l}_{h}") for h in range(2)] for l in range(2)]

        relaid = [[sem(f"relaid{l}_{h}") for h in range(2)] for l in range(2)]
        top_max, top_found, exp_done, replaced, inverse, kept_top, prob_ready = (
            sem(n) for n in ("top_max", "top_found", "exp_done", "replaced", "inverse", "kept_top", "prob_ready"))
        prob_saved = sem("prob_saved")
        transposed, pool_mm, pool_kept, pool_tr, pool_read = (
            sem(n) for n in ("transposed", "pool_mm", "pool_kept", "pool_tr", "pool_read"))
        tt_ready = [sem(f"tt_ready{j}") for j in range(2)]
        ew_dma, hid_mm, hid_act, eo_mm, outt_ready, lh_zero, lh_tr, lh_ready, lhg_ready = (
            sem(n) for n in ("ew_dma", "hid_mm", "hid_act", "eo_mm", "outt_ready", "lh_zero", "lh_tr", "lh_ready", "lhg_ready"))
        rdma, rnn_t, rnn_w_ready, bn_pe, bn_dve, bn_step, rnn_ready = (
            sem(n) for n in ("rdma", "rnn_t", "rnn_w_ready", "bn_pe", "bn_dve", "bn_step", "rnn_ready"))
        bn_std = sem("bn_std")
        pool_done = sem("pool_done")
        passed = sem("passed")
        step_mm, step_y, seg_done, x2_in, added, out_st = (
            sem(n) for n in ("step_mm", "step_y", "seg_done", "x2_in", "added", "out_st"))

        SPREAD = (PS[4], PS[7])
        STEPS = [H - 1, H - 2, W - 1, W - 2]
        LINES0 = [1, H, 2 * H - 1, 2 * H + W - 2]
        STEPS0 = [0, H - 1, 2 * H - 3, 2 * H + W - 4]
        LINES = 2 * H + 2 * W - 4
        assert LINES == LINES0[3] + STEPS[3]

        def nat(t):
            v = t if len(t.shape) == 3 else t.rearrange("b c h w -> b c (h w)")
            return v.rearrange("(h b) c t -> h c b t", h=2)

        def nat_all(t):
            return t.rearrange("b c t -> c b t")

        def rows_view(p, h):
            return img[p[0]:p[1], h * HALF:(h + 1) * HALF].rearrange("p (b r j) -> p b r j", r=H, j=WP)

        def cols_view(p, h):
            return img[p[0]:p[1], h * HALF:(h + 1) * HALF].rearrange("p (b r j) -> p b r j", r=W, j=HP)

        LOW, HIGH, ALL = (0, 64), (64, 128), (0, 128)
        SIDE = (LOW, HIGH)

        def shape_of(k):
            rows = k < 2
            view, n, pairs = (rows_view, H, WP) if rows else (cols_view, W, HP)
            if k % 2 == 0:
                return view, int(rows), (lambda s: s), (lambda s: s + 1), pairs
            return view, int(rows), (lambda s: s * -1 + (n - 1)), (lambda s: s * -1 + (n - 2)), pairs

        def each_step(eng, k, step):
            n, first = STEPS[k], sum(STEPS[:k])
            with eng.Fori(0, n // 2) as j:
                for u in range(2):
                    step(j * 2 + u, [PS[2 * ((first + u) % 2) + h] for h in range(2)])
            if n % 2:
                step(n - 1, [PS[2 * (first % 2) + h] for h in range(2)])

        SRC = [nat(x), nat(x), nat(t_dram), nat(x1_dram)]
        DST = [None, nat(t_dram), nat(x1_dram), nat(x2_dram)]
        EPS = [EPS_C, EPS_T, EPS_C, EPS_T]
        N2 = 2 * NCH

        def index(u, k):
            g, d, v = u
            return g * N2 + (d * N2 + v * NCH + k)

        def ring_use(u, k):
            g, d, v = u
            return g * (N2 // RING) + (d * N2 + v * NCH + k) // RING

        def units_before(u):
            g, d, v = u
            return g * 2 + (2 * d + v)

        def batch(i, u):
            g, d, v = u
            return g * 2 + (2 * d + v) if i != 2 else g * -2 + (HB - 1 - 2 * d - v)

        SCALE = NCH + 5
        PIECES = 2

        def behind(n, lag, units):
            k, j = n - lag, 0
            while k < 0:
                k, j = k + NCH, j + 1
            return units[j], k, (units + (None,))[j + 1]

        def pipeline(eng, i, phase, ending=None):
            if i == 1:
                with eng.Fori(0, NG) as g:
                    phase(((g, 0, 0), None, None))
                    phase(((g, 0, 1), (g, 0, 0), None))
                    phase((None, (g, 0, 1), (g, 0, 0)))
                    phase((None, None, (g, 0, 1)))
                    ending(g)
            else:
                last = NG - 1
                phase(((0, 0, 0), None, None))
                phase(((0, 0, 1), (0, 0, 0), None))
                with eng.Fori(0, NG - 1) as g:
                    phase(((g, 1, 0), (g, 0, 1), (g, 0, 0)))
                    phase(((g, 1, 1), (g, 1, 0), (g, 0, 1)))
                phase((None, (last, 0, 1), (last, 0, 0)))
                phase((None, None, (last, 0, 1)))

        def stat_rows(v, k):
            return 2 * v + k % 2, 2 * (k // 2)

        def token_pieces(k):
            a, b = k * CH, (k + 1) * CH
            if b <= SLOT:
                return [(0, 0, a, CH)]
            if a >= SLOT:
                return [(0, 1, a - SLOT, CH)]
            return [(0, 0, a, SLOT - a), (SLOT - a, 1, 0, b - SLOT)]

        def slot_tokens(z, b, a, m):
            return slots[:, z, ds(b, 1), a:a + m].rearrange("p b t -> p (b t)")

        def whole(b):
            return slots[:, :, ds(b, 1), :].rearrange("p z b t -> p z (b t)")

        spare = slots[:, :, HB, :]

        def own(eng):
            eng.sem_inc(passed, 1)

        NIT = S // (BODY * SEG)
        HIT = NIT // 2
        block = ctx.enter_context(nc.Block())

        def sp_norm(sp, i, meanwhile=None):
            st = ln[i]

            def turn(g, final=False):
                at = [batch(i, (g, v // 2, v % 2)) for v in range(2 if final else 3)]
                if not final:
                    at = [sp.snap(b) for b in at]

                def chunk(t, n):
                    v, k = n // NCH, n % NCH
                    return t[:, :, ds(at[v], 1), k * CH:(k + 1) * CH].rearrange("h c b t -> h c (b t)")

                for n in range(N2):
                    r = n % RING
                    if DST[i] is None:
                        sp.wait_ge(st.centred, g * N2 + (n + 1))
                        own(sp)
                    else:
                        sp.wait_ge(st.summed, g * N2 + (n + 1))
                        sp.dma_start(chunk(DST[i], n), sums[:, r * CH:(r + 1) * CH]).then_inc(st.stored[r], 16)
                    if not final or n + RING < N2:
                        sp.dma_start(ring[:, r * CH:(r + 1) * CH], chunk(SRC[i], n + RING)).then_inc(st.loaded[r], 16)

            for r in range(RING):
                sp.dma_start(ring[:, r * CH:(r + 1) * CH],
                             SRC[i][:, :, batch(i, (0, 0, 0)), r * CH:(r + 1) * CH]).then_inc(st.loaded[r], 16)
            with sp.Fori(0, NG - 1) as g:
                turn(g)
            turn(NG - 1, final=True)
            if meanwhile:
                meanwhile()
            if DST[i] is not None:
                for r in range(RING):
                    sp.wait_ge(st.stored[r], 16 * NG * (N2 // RING))

        def load_w1(sp, e0, n):
            slot = slots[0:D1, 0, 1 + 2 * (e0 // 7), 0:n * HID] if e0 < 28 else slots[0:D1, 1, 3 if n > 1 else 5, 16 * C:16 * C + n * HID]
            sp.dma_start(slot.rearrange("p (e h) -> p e h", e=n),
                         weight1[e0:e0 + n].rearrange("e d h -> d e h")).then_inc(ew_dma, 16)

        def load_b2(sp, e0, n):
            sp.dma_start(b2_at(e0, n).rearrange("p (e o) -> p e o", e=n),
                         weight2[e0:e0 + n, HID:D2, :].rearrange("e p o -> p e o")).then_inc(ew_dma, 16)

        def load_w2(sp, part):
            c, e0 = part // 2, 16 * (part % 2)
            sp.dma_start(slots[:, 1, 1 + 2 * part, 0:16 * C].rearrange("p (e o) -> p e o", e=16),
                         weight2[e0:e0 + 16, c * 128:(c + 1) * 128, :].rearrange("e p o -> p e o")).then_inc(ew_dma, 16)

        def early_weights(sp):
            sp.wait_ge(ln[1].copied, NG * N2)
            for part in range(1, 4):
                load_w1(sp, 7 * part, 7)
                load_w2(sp, part)
            load_w1(sp, 28, 3)
            load_w1(sp, 31, 1)
            for e0, n in ((0, 12), (12, 4), (28, 4)):
                load_b2(sp, e0, n)
            sp.wait_ge(prob_ready, 2 * NG)
            load_w1(sp, 0, 7)
            load_w2(sp, 0)
            load_b2(sp, 16, 12)

        def sp_taps(sp, l):
            for q in range(4):
                sp.dma_start(half(wraw, q % 2)[:, (q // 2) * C * KT:(q // 2 + 1) * C * KT],
                             conv_w[4 * l + q].rearrange("o i a b -> o (i a b)")).then_inc(wdma[l], 16)

        @block.sync
        def _(sp):
            sp.dma_start(graw[:, :], gate_w).then_inc(setup_dma, 16)
            for q in range(4):
                sp.dma_start(gbias[q * E:(q + 1) * E, :], gate_b.rearrange("(e a) -> e a", a=1)).then_inc(setup_dma, 16)
            sp_taps(sp, 0)
            sp.dma_start(wraw_r[:, 0:64], rnn_w).then_inc(rdma, 16)
            sp.dma_start(wraw_r[:, 64:128], rnn_v).then_inc(rdma, 16)
            sp.dma_start(gb[:, 0:1], gamma.rearrange("(e a) -> e a", a=1)).then_inc(rdma, 16)
            sp.dma_start(gb[:, 1:2], beta.rearrange("(e a) -> e a", a=1)).then_inc(rdma, 16)
            sp_norm(sp, 0)
            sp_norm(sp, 1, meanwhile=lambda: early_weights(sp))
            sp.wait_ge(pool_read, NG)
            sp_taps(sp, 1)
            sp_norm(sp, 2)
            sp_norm(sp, 3)
            sp.wait_ge(rnn_ready, 1)
            with sp.Fori(0, NIT) as i:
                sp.dma_start(x2b, nat_all(x2_dram)[:, :, ds(i * (BODY * SEG), BODY * SEG)]).then_inc(x2_in, 16)
                sp.wait_ge(added, i * BODY + 2 * BODY)
                sp.dma_start(nat_all(out.rearrange("b c h w -> b c (h w)"))[:, :, ds(i * (BODY * SEG), BODY * SEG)],
                             ob).then_inc(out_st, 16)
            sp.wait_ge(out_st, 16 * (NIT + 1))

        @block.gpsimd
        def _(pool):
            done = [0]

            def alone(ins):
                done[0] += 1
                ins.then_inc(pool_done, 1)
                pool.wait_ge(pool_done, done[0])

            for buf, value in ((ident, 0.0), (average, 0.0), (fold, 0.0), (gate, 0.0), (wbd, 0.0), (taps, 0.0), (ones, 1.0),
                               (pooled, 1.0)):
                alone(pool.memset(buf[:, :], value))
            for n, value in enumerate(EPS + [EPS_BN]):
                alone(pool.memset(eps[:, n:n + 1], value))
            for h in range(2):
                alone(pool.memset(half(average, h)[:, h * 64:(h + 1) * 64], 1.0 / C))
            for base in (0, 64, -64):
                alone(pool.affine_select(out=fold[:, :], in_=fold[:, :], compare_op=ALU.not_equal, fill=0.5, base=base,
                                         pattern=[[-1, 128]], channel_multiplier=1))
            pool.affine_select(out=ident[:, :], in_=ident[:, :], compare_op=ALU.not_equal, fill=1.0, base=0,
                               pattern=[[-1, 128]], channel_multiplier=1).then_inc(consts, 1)
            alone(pool.memset(pick[:, :], 0.0))
            for h in range(2):
                alone(pool.memset(half(pick, h)[:, 126 + h:127 + h], 1.0 / C))
            ones_at = sums[:, 0:5 * 128]
            alone(pool.memset(ones_at, 0.0))
            pool.sem_inc(pick_ready, 1)
            for v in range(2):
                for k in range(NCH):
                    for h in range(2):
                        q, p = stat_rows(v, k)
                        part = ones_at[:, p * 64 + h * 64:p * 64 + (h + 1) * 64]
                        alone(pool.affine_select(out=part, in_=part, compare_op=ALU.not_equal, fill=1.0, base=-(32 * q + p + h),
                                                 pattern=[[0, 64]], channel_multiplier=1))
            pool.tensor_copy(spread[:, :], ones_at).then_inc(spread_ready, 1)
            with pool.Fori(0, NG) as g:
                pool.wait_ge(prob_ready, g * 2 + 2)
                own(pool)
                pool.tensor_copy(whole(2 * g), spare).then_inc(prob_saved, 1)
            pool.wait_ge(eo_mm, 1)
            pool.memset(lh, 0.0).then_inc(lh_zero, 1)
            pool.wait_ge(lh_ready, 1)
            pool.tensor_copy(lhg[:, :], lh[:, (NG - 1) * 256:NG * 256]).then_inc(lhg_ready, 1)
            with pool.Fori(0, NG - 1) as g:
                pool.wait_ge(ln[2].summed, g * N2 + N2)
                own(pool)
                pool.tensor_copy(lhg[:, :], lh[:, ds(g * -256 + (NG - 2) * 256, 256)]).then_inc(lhg_ready, 1)

        def pe_taps(pe, l):
            pe.wait_ge(wdma[l], 64)
            wk = wraw.rearrange("p (a i k) -> p a k i", a=2, k=KT)
            for a in range(2):
                for k in range(KT):
                    if a == 1 and k % 4 == 0:
                        pe.wait_ge(wcp[l], k // 4 + 1)
                    last = pe.transpose(PS[4 + k // 4][0:64, (k % 4) * 128:(k % 4 + 1) * 128], wk[:, a, k, :], ident[:, :])
                    if k % 4 == 3 or k == KT - 1:
                        last.then_inc(wtr[l], 1)

        def pe_norm(pe, i, before=None, after=None, ending=None):
            st = ln[i]
            source = sums if DST[i] is not None else ring

            def phase(units):
                for n in range(NCH):
                    u, k, prev = behind(n, 0, units)
                    if u:
                        r = k % RING
                        if before:
                            for m in ((0, 1) if k == 0 else (k + 1,)):
                                if m < NCH:
                                    before(u, m)
                        if i == 0:
                            pe.wait_ge(st.loaded[r], (ring_use(u, k) + 1) * 16)
                        else:
                            pe.wait_ge(st.summed, index(u, k + 1))
                        if k >= RING or prev:
                            pe.wait_ge(st.kept, index(u, k - RING + 1))
                        pe.matmul(PS[r][:, 0:CH], centre[:, :], source[:, r * CH:(r + 1) * CH], start=True, stop=True
                                  ).then_inc(st.centred, 1)
                    u, k, prev = behind(n, SCALE, units)
                    if u:
                        q, p = stat_rows(u[2], k)
                        if i == 0 and k == 0 and not (prev or units[0][1]):
                            pe.wait_ge(spread_ready, 1)
                        if k == 0:
                            pe.wait_ge(st.rstd, units_before(u) * PIECES + PIECES)
                        if k >= 2 or prev:
                            pe.wait_ge(st.normed, index(u, k - 1))
                        for part in range(2):
                            last = pe.matmul(SPREAD[(u[2] * NCH + k) % 2][:, 0:CH], spread[32 * q:32 * q + 32, p * 64:p * 64 + 128],
                                             rparts[32 * q:32 * q + 32, part * CH:(part + 1) * CH],
                                             start=(part == 0), stop=(part == 1))
                        last.then_inc(st.spread, 1)
                    u, k, prev = behind(n, 2, units)
                    if u:
                        q, p = stat_rows(u[2], k)
                        c0 = 126 - 32 * (q % 2) - p
                        j = (u[2] * NCH + k) % 2
                        pe.wait_ge(st.squared, index(u, k + 1))
                        pe.matmul(PS[3][u[2] * 64:(u[2] + 1) * 64, 0:CH], pick[:, c0:c0 + 64], sq[:, j * CH:(j + 1) * CH],
                                  start=(k == 0), stop=(k == NCH - 1)).then_inc(st.var, 1)
                    u, k, prev = behind(n, SCALE + 2, units)
                    if u and after:
                        after(u, k, prev)

            pipeline(pe, i, phase, ending)

        def pe_rows(pe, l, k):
            def step(s, banks):
                for h in range(2):
                    acc = banks[h][:, 0:HB * WP].rearrange("p (b j) -> p b j", b=HB)

                    def products(tap_part, line_part):
                        for d in OFFS:
                            t0 = (k * NO + d + 2) * 128
                            ins = pe.matmul(acc, taps_part[tap_part][:, t0:t0 + 128], line_pairs(h, line_part, d),
                                            start=(tap_part == line_part == 0 and d == OFFS[0]),
                                            stop=(line_part == 1 and d == OFFS[-1]))
                        return ins

                    pe.wait_ge(hi[l][h], s + LINES0[k])
                    products(0, 0)
                    products(1, 0)
                    pe.wait_ge(lo[l][h], s + LINES0[k])
                    products(0, 1).then_inc(conv[l][h], 1)

            each_step(pe, k, step)

        def pe_columns(pe, l, k):
            view, s0, src, _, pairs = shape_of(k)
            with pe.Fori(0, STEPS[k]) as s:
                at = pe.snap(src(s))
                for h in range(2):
                    acc = PS[h][:, 0:HB * pairs].rearrange("p (b j) -> p b j", b=HB)
                    v = view(ALL, h)
                    pe.wait_ge(state[l][h], s + LINES0[k])
                    for n, d in enumerate(OFFS):
                        lo, hi = max(0, -d), min(pairs, pairs - d)
                        last = pe.matmul(acc[:, :, lo:hi], taps[:, (k * NO + d + 2) * 128:(k * NO + d + 3) * 128],
                                         v[:, s0:s0 + HB, ds(at, 1), lo + d:hi + d].rearrange("p b r j -> p b (r j)"),
                                         start=(n == 0), stop=(n == NO - 1))
                    last.then_inc(conv[l][h], 1)

        def pe_layer(pe, l):
            pe.wait_ge(taps_lo[l], 1)
            pe_rows(pe, l, 0)
            pe_rows(pe, l, 1)
            pe_columns(pe, l, 2)
            pe_columns(pe, l, 3)

        def logits(pe, u, k, prev):
            g, _, v = u
            if v == 0:
                return
            if k >= 2:
                pe.wait_ge(ln[1].taken, g * NCH + (k - 1))
            pe.wait_ge(ln[1].normed, index(u, k + 1))
            for v in range(2):
                last = pe.matmul(PS[5 + k % 2][:, 0:CH], gate[:, v * 128:(v + 1) * 128],
                                 xl[:, v * S + k * CH:v * S + (k + 1) * CH], start=(v == 0), stop=(v == 1))
            last.then_inc(ln[1].mixed, 1)

        def pooling(pe, g):
            for c in range(NTC + 2):
                if c in (0, NTC // 2):
                    pe.wait_ge(prob_ready, g * 2 + (c // (NTC // 2) + 1))
                    own(pe)
                if c < NTC:
                    bank = PS[5 + c % RING]
                    if c >= RING:
                        pe.wait_ge(tt_ready[(c - RING) % 2], g * (NTC // 2) + ((c - RING) // 2 + 1))
                    pe.transpose(bank[0:TC, 0:128], slots[:, c // (NTC // 2), HB, (c % (NTC // 2)) * TC:(c % (NTC // 2) + 1) * TC], ident[:, :])
                    for v in range(2):
                        last = pe.transpose(bank[0:TC, 128 + v * 128:256 + v * 128],
                                            xl[:, v * S + c * TC:v * S + (c + 1) * TC], ident[:, :])
                    last.then_inc(transposed, 1)
                if c >= 2:
                    m = c - 2
                    pe.wait_ge(tt_ready[m % 2], g * (NTC // 2) + (m // 2 + 1))
                    o = (m % RING) * 384
                    for v in range(2):
                        last = pe.matmul(PS[0][v * 64:(v + 1) * 64, 0:128], tt[:, o + v * 64:o + (v + 1) * 64],
                                         tt[:, o + 128 + v * 128:o + 256 + v * 128], start=(m == 0), stop=(m == NTC - 1))
                    last.then_inc(pool_mm, 1)
            pe.wait_ge(pool_kept, g + 1)
            own(pe)
            pe.transpose(PS[1][:, 0:128], tt_pool, ident[:, :]).then_inc(pool_tr, 1)
            pe.wait_ge(pool_read, g + 1)

        def mixture(pe, u, k):
            g, d, v = u
            n = v * NCH + k
            if n == 0:
                pe.wait_ge(lhg_ready, g + (d + 1))
            if n >= 2:
                pe.wait_ge(ln[2].summed, index(u, k - 1))
            for o, z, a, m in token_pieces(k):
                last = pe.matmul(PS[5 + n % 2][:, o:o + m], lhg[:, (1 - v) * 128:(2 - v) * 128],
                                 slot_tokens(z, g * -2 + (HB - 2 - 2 * d), a, m), start=True, stop=True)
            last.then_inc(ln[2].mixed, 1)

        def rnn_input(pe, u, k, prev):
            n = u[2] * NCH + k
            if k >= 2 or prev:
                pe.wait_ge(ln[3].taken, index(u, k - 1))
            pe.wait_ge(ln[3].normed, index(u, k + 1))
            for o, z, a, m in token_pieces(k):
                last = pe.matmul(PS[5 + n % 2][:, o:o + m], wbd[:, :], slot_tokens(z, batch(3, u), a, m), start=True, stop=True)
            last.then_inc(ln[3].mixed, 1)

        def fill_input(pe, bank, h, z, t0, s, c0, w, first):
            acc = PS[bank][0:64, 0:SEG * B].rearrange("p (t b) -> p b t", b=B)
            images = img[:, :].rearrange("p (z n) -> p z n", z=2)[:, ds(z, 1), s * SEG:s * SEG + HB * SLOT]
            tok = images.rearrange("p z (b t) -> p (z b) t", b=HB)[:, :, ds(t0 + c0, w)]
            pe.matmul(acc[:, h * HB:(h + 1) * HB, c0:c0 + w], wsc[h], tok, start=first, stop=True, skip_group_check=True)

        @block.tensor
        def _(pe):
            pe.wait_ge(consts, 1)
            pe.wait_ge(setup_dma, 80)
            pe.transpose(PS[7][0:C, 0:E], graw[:, :], ident[0:E, 0:E]).then_inc(gate_t, 1)
            pe.wait_ge(rdma, 64)
            pe.wait_ge(gate_ready, 1)
            for a in range(2):
                last = pe.transpose(PS[7][0:64, 64 + a * 64:128 + a * 64], wraw_r[:, a * 64:(a + 1) * 64], ident[0:64, 0:64])
            last.then_inc(rnn_t, 1)
            pe_taps(pe, 0)
            pe.wait_ge(wcp[0], 6)
            pe.wait_ge(centre_ready, 1)
            pe.wait_ge(pick_ready, 1)
            pe_norm(pe, 0)
            pe_layer(pe, 0)
            pe.wait_ge(gate_ready, 1)
            pe_norm(pe, 1, after=lambda *at: logits(pe, *at), ending=lambda g: pooling(pe, g))

            pe.wait_ge(ew_dma, 16 * 14)
            pv = pooled[:, :].rearrange("p (b e) -> p e b", e=E)
            for e in range(E):
                for c in range(2):
                    last = pe.matmul(PS[e // 16][:, (e % 16) * 32 + c * 16:(e % 16) * 32 + (c + 1) * 16],
                                     w1_at(e)[:, c * 128:(c + 1) * 128], pv[:, e, :], start=True, stop=True)
                if e % 16 == 15:
                    last.then_inc(hid_mm, 1)
            pe_taps(pe, 1)
            eo = PS[2][0:64, :].rearrange("p (b e) -> p e b", e=E)
            for e in range(E):
                if e % 16 == 0:
                    pe.wait_ge(hid_act, e // 16 + 1)
                for c in range(2):
                    pe.matmul(eo[:, e, :], w2_at(c, e), hidden[:, e * 32 + c * 16:e * 32 + (c + 1) * 16],
                              start=(c == 0), stop=False)
                last = pe.matmul(eo[:, e, :], b2_at(e), ones[:, 0:B], start=False, stop=True)
            last.then_inc(eo_mm, 1)
            pe.wait_ge(outt_ready, 1)
            for g in range(NG):
                last = pe.transpose(PS[3][:, g * 64:(g + 1) * 64], outt[:, g * 128:(g + 1) * 128], ident[0:64, 0:64])
            last.then_inc(lh_tr, 1)
            pe.wait_ge(wcp[1], 6)
            pe_norm(pe, 2, before=lambda u, k: mixture(pe, u, k))
            pe_layer(pe, 1)
            pe.wait_ge(rnn_w_ready, 1)
            pe_norm(pe, 3, after=lambda *at: rnn_input(pe, *at))

            pe.wait_ge(bn_dve, 1)
            pe.matmul(PS[7][:, 0:1], fold[:, :], bnm[:, 0:1], start=True, stop=True).then_inc(bn_pe, 1)
            pe.wait_ge(bn_dve, 2)
            pe.matmul(PS[7][:, 2:3], fold[:, :], bnm[:, 3:4], start=True, stop=True).then_inc(bn_pe, 1)
            pe.wait_ge(bn_dve, 3)
            pe.transpose(PS[7][0:64, 64:128], wrow, ident[0:64, 0:64])
            pe.transpose(PS[7][0:1, 128:192], bnm[0:64, 8:9], ident[0:64, 0:64]).then_inc(bn_pe, 1)
            pe.wait_ge(rnn_ready, 1)

            with pe.Fori(0, 2) as z:
                for h in range(2):
                    fill_input(pe, 0, h, z, 0, 0, 0, SEG, h == 0)
                with pe.Fori(0, HIT) as j:
                    t0 = j * (BODY * SEG)
                    for s in range(BODY):
                        for t in range(SEG):
                            n = s * SEG + t
                            if n == 0:
                                pe.wait_ge(step_y, BODY * SEG)
                                pe.sem_clear(step_y)
                            else:
                                pe.wait_ge(step_y, n)
                            if t == 0:
                                pe.sem_inc(seg_done, 1)
                            prev = yb[:, s, :, t - 1] if t else yb[:, (s - 1) % BODY, :, SEG - 1]
                            for c in range(2):
                                last = pe.matmul(PS[s % 2][c * 32:(c + 1) * 32, t * B:(t + 1) * B], vt[:, c * 32:(c + 1) * 32],
                                                 prev, start=False, stop=True, skip_group_check=True)
                            last.then_inc(step_mm, 1)
                            if t < 20:
                                fill_input(pe, (s + 1) % 2, t // 10, z, t0, s + 1, (t % 10) * 3, 3, t == 0)
            pe.wait_ge(step_y, BODY * SEG)
            pe.sem_inc(seg_done, 1)

        def split_taps(act, l):
            act.wait_ge(taps_ready[l], 1)
            act.wait_ge(ln[2 * l].normed, NG * N2)
            act.activation(taps_part[0], taps[:, 0:2 * NO * 128], ACT.Copy).then_inc(taps_hi[l], 1)

        def act_relayout(act, l):
            relayout(act, l, 1, lambda o, a: act.activation(o, a, ACT.Copy))

        def relayout(eng, l, h, move):
            eng.wait_ge(state[l][h], LINES0[2] - 1)
            eng.wait_ge(lo[l][h], LINES0[2] - 1)
            eng.sem_inc(relaid[l][h], 1)
            with eng.Fori(0, HB) as b:
                eng.wait_ge(relaid[l][h], b + 1)
                own(eng)
                for hp in range(2):
                    for wp in range(2):
                        dst = cols_view(SIDE[hp], h)[:, ds(b, 1), wp::2, :].rearrange("p b w j -> p (b w) j")
                        src = rows_view(SIDE[wp], h)[:, ds(b + 1, 1), hp::2, :].rearrange("p b r j -> p j (b r)")
                        last = move(dst, src)
                last.then_inc(relaid[l][h], 1)
            eng.wait_ge(relaid[l][h], HB + 1)
            eng.sem_inc(state[l][h], 1)

        def act_norm(act, i, copy=False, ending=None):
            st = ln[i]

            def natural(u, k):
                r = k % RING
                if k >= RING or u[1] or u[2]:
                    act.wait_ge(st.stored[r], ring_use(u, k) * 16)
                    own(act)
                for h in range(2):
                    for hp in range(2):
                        dst = half(sums, h)[:, r * CH:(r + 1) * CH].rearrange("p (r w) -> p r w", w=W)[:, hp::2, :]
                        src = cols_view(SIDE[hp], h)[:, ds(batch(i, u), 1), :, k * (CH_ROWS // 2):(k + 1) * (CH_ROWS // 2)]
                        last = act.activation(dst, src.rearrange("p b w j -> p j (b w)"), ACT.Copy)
                last.then_inc(st.copied, 1)

            def phase(units):
                for n in range(NCH):
                    u, k, prev = behind(n, 0, units)
                    if u and copy:
                        natural(u, k)
                    u, k, prev = behind(n, 1, units)
                    if u:
                        j = (u[2] * NCH + k) % 2
                        act.wait_ge(st.centred, index(u, k + 1))
                        if k >= 2 or prev:
                            act.wait_ge(st.var, index(u, k - 1))
                        act.activation(sq[:, j * CH:(j + 1) * CH], PS[k % RING][:, 0:CH], ACT.Square).then_inc(st.squared, 1)
                        act.activation(xl[:, u[2] * S + k * CH:u[2] * S + (k + 1) * CH], PS[k % RING][:, 0:CH], ACT.Copy
                                       ).then_inc(st.kept, 1)
                    u, k, prev = behind(n, 3, units)
                    if u and k == NCH - 1:
                        act.wait_ge(st.var, index(u, NCH))
                        act.activation(half(rstd, u[2]), half(PS[3], u[2])[:, 0:CH], ACT.Sqrt, bias=half(eps, u[2])[:, i:i + 1]
                                       ).then_inc(st.std, 1)

            pipeline(act, i, phase, ending)

        def take_logits(act, g, k):
            act.wait_ge(ln[1].mixed, g * NCH + (k + 1))
            for o, z, a, m in token_pieces(k):
                last = act.activation(spare[:, z, a:a + m], PS[5 + k % 2][:, o:o + m], ACT.Identity, bias=gbias[:, 0:1])
            last.then_inc(ln[1].taken, 1)

        def route(act, g):
            for k in range(NCH):
                take_logits(act, g, k)
            act.activation(warm[:, :], ones[0:1, 0:1], ACT.Exp)
            act.wait_ge(top_found, g + 1)
            own(act)
            act.activation(whole(2 * g), spare, ACT.Exp, bias=stat[:, 0:1], accum_out=stat[:, 1:2]).then_inc(exp_done, 1)
            sums_stored(act, g)
            for c in range(1, NTC, 2):
                take_transposed(act, g, c, lambda o, a: act.activation(o, a, ACT.Copy))
            act.wait_ge(pool_mm, g * NTC + NTC)
            act.activation(tt_pool, PS[0][:, 0:128], ACT.Copy).then_inc(pool_kept, 1)
            act.wait_ge(pool_tr, g + 1)
            for v in range(2):
                for h in range(2):
                    last = act.activation(pooled[0:C, ds(g * 128 + (2 * v + h) * E, E)],
                                          half(PS[1], h)[:, v * 64 + h * E:v * 64 + (h + 1) * E], ACT.Copy)
            last.then_inc(pool_read, 1)
            act.wait_ge(prob_saved, g + 1)
            own(act)

        def sums_stored(eng, g):
            for r in range(RING):
                eng.wait_ge(ln[1].stored[r], g * (16 * N2 // RING) + 16 * N2 // RING)
            own(eng)

        def take_transposed(eng, g, c, move):
            eng.wait_ge(transposed, g * NTC + (c + 1))
            if c >= RING:
                eng.wait_ge(pool_mm, g * NTC + (c - RING + 1))
            move(tt[:, (c % RING) * 384:(c % RING + 1) * 384], PS[5 + c % RING][0:TC, 0:384]).then_inc(tt_ready[c % 2], 1)

        @block.scalar
        def _(act):
            act.wait_ge(setup_dma, 80)
            act.wait_ge(consts, 1)
            act.wait_ge(taps_ready[0], 1)
            act_norm(act, 0)
            split_taps(act, 0)
            act_relayout(act, 0)
            for h in range(2):
                act.wait_ge(state[0][h], LINES)
            act_norm(act, 1, copy=True, ending=lambda g: route(act, g))
            for j in range(2):
                act.wait_ge(hid_mm, j + 1)
                act.activation(hidden[:, j * 512:(j + 1) * 512], PS[j][:, :], ACT.Gelu).then_inc(hid_act, 1)
            act.wait_ge(taps_ready[1], 1)
            act_norm(act, 2)
            split_taps(act, 1)
            act_relayout(act, 1)
            for h in range(2):
                act.wait_ge(state[1][h], LINES)
            for r in range(RING):
                act.wait_ge(ln[2].stored[r], 16 * NG * (N2 // RING))
            act_norm(act, 3, copy=True)
            act.wait_ge(bn_pe, 2)
            act.activation(bnm[0:64, 4:5], PS[7][0:64, 2:3], ACT.Sqrt, bias=eps[0:64, 4:5]).then_inc(bn_std, 1)
            act.wait_ge(rnn_ready, 1)
            act.activation(warm[:, :], ones[0:1, 0:1], ACT.Sigmoid)
            with act.Fori(0, NIT) as i:
                for s in range(BODY):
                    act.wait_ge(added, i * BODY + (s + 1))
                    for t in range(SEG):
                        n = s * SEG + t
                        act.wait_ge(step_mm, n + 1)
                        if n == BODY * SEG - 1:
                            act.sem_clear(step_mm)
                        act.activation(yb[0:64, s, :, t], PS[s % 2][0:64, t * B:(t + 1) * B], ACT.Sigmoid).then_inc(step_y, 1)

        def dve_taps(dve, l):
            for a in range(2):
                for j, (k0, k1) in enumerate(((0, 4), (4, 8), (8, 9))):
                    dve.wait_ge(wtr[l], a * 3 + j + 1)
                    dve.tensor_copy(wt[:, a, k0:k1, :, :],
                                    PS[4 + j][0:64, 0:(k1 - k0) * 128].rearrange("p (k s o) -> p k s o", s=2, o=64)
                                    ).then_inc(wcp[l], 1)

            dve.wait_ge(wcp[l], 6)
            for q in range(4):
                for ip in range(2):
                    for op in range(2):
                        d0, d1 = (-2, 2) if ip == op else (-1, 2) if ip < op else (-2, 1)
                        k0 = 2 * d0 + 4 + ip - op
                        dst = half(taps, ip)[:, q * NO * 128:(q + 1) * NO * 128].rearrange("p (d o c) -> p d o c", d=NO, o=2)
                        last = dve.tensor_copy(dst[:, d0 + 2:d1 + 3, op, :], wt[:, q // 2, k0:k0 + 2 * (d1 - d0) + 1:2, q % 2, :])
            last.then_inc(taps_ready[l], 1)
            dve.wait_ge(taps_ready[l], 1)

        def dve_norm(dve, i, later=None, ending=None):
            st = ln[i]

            def total(u, k):
                r = k % RING
                dve.wait_ge(st.loaded[r], (ring_use(u, k) + 1) * 16)
                if i == 2:
                    if k >= RING or u[1] or u[2]:
                        dve.wait_ge(st.stored[r], ring_use(u, k) * 16)
                    dve.wait_ge(st.mixed, index(u, k + 1))
                    add = PS[5 + (u[2] * NCH + k) % 2][:, 0:CH]
                else:
                    dve.wait_ge(st.copied, index(u, k + 1))
                    add = sums[:, r * CH:(r + 1) * CH]
                dve.tensor_tensor(sums[:, r * CH:(r + 1) * CH], add, ring[:, r * CH:(r + 1) * CH], ALU.add).then_inc(st.summed, 1)

            def scale(u, k, at):
                c0 = u[2] * S + k * CH
                xc, rs = xl[:, c0:c0 + CH], SPREAD[(u[2] * NCH + k) % 2][:, 0:CH]
                dve.wait_ge(st.spread, index(u, k + 1))
                if i in (0, 2):
                    for h in range(2):
                        for wp in range(2):
                            dst = rows_view(SIDE[wp], h)[:, ds(at, 1), k * CH_ROWS:(k + 1) * CH_ROWS, :]
                            parity = (lambda t: half(t, h).rearrange("p (r j e) -> p r j e", j=WP, e=2)[:, :, :, wp])
                            last = dve.tensor_tensor(dst.rearrange("p b r j -> p (b r) j"), parity(xc), parity(rs), ALU.mult)
                elif i == 1:
                    last = dve.tensor_tensor(xc, xc, rs, ALU.mult)
                else:
                    for o, z, a, c in token_pieces(k):
                        last = dve.tensor_tensor(slot_tokens(z, batch(i, u), a, c), xc[:, o:o + c], rs[:, o:o + c], ALU.mult)
                last.then_inc(st.normed, 1)

            def phase(units):
                at = {}
                for u in units[1:]:
                    if u and i in (0, 2):
                        at[u[1:]] = batch(i, u) + 1 if isinstance(u[0], int) else dve.snap(batch(i, u) + 1)
                for n in range(NCH):
                    v, piece = None, 0
                    for p in range(PIECES):
                        u, k, _ = behind(n, 4 + p, units)
                        if u and k == NCH - 1:
                            v, piece = u, p
                    if v:
                        w0, w1 = CH * piece // PIECES, CH * (piece + 1) // PIECES
                        done = units_before(v) * PIECES + (piece + 1)
                        r0, high, low = half(rstd, v[2])[:, w0:w1], half(rparts, v[2])[:, w0:w1], half(rparts, v[2])[:, CH + w0:CH + w1]
                        dve.wait_ge(st.std, units_before(v) + 1)
                        dve.reciprocal(r0, r0).then_inc(st.inverse, 1)
                    u, k, _ = behind(n, 0, units)
                    if u and i > 0:
                        total(u, k)
                    u, k, _ = behind(n, SCALE + 1, units)
                    if u:
                        scale(u, k, at.get(u[1:]))
                    if v:
                        dve.wait_ge(st.inverse, done)
                        own(dve)
                        dve.tensor_copy(high, r0).then_inc(st.high, 1)
                    u, k, _ = behind(n, SCALE + 3, units)
                    if u and later:
                        later(u, k)
                    if v:
                        dve.wait_ge(st.high, done)
                        own(dve)
                        dve.tensor_tensor(low, r0, high, ALU.subtract).then_inc(st.rstd, 1)

            pipeline(dve, i, phase, ending)

        def dve_route(dve, g):
            dve.wait_ge(ln[1].taken, g * NCH + NCH)
            own(dve)
            dve.max(top8[:, :], spare).then_inc(top_max, 1)
            dve.wait_ge(top_max, g + 1)
            dve.tensor_scalar(stat[:, 0:1], top8[:, 0:1], -1.0, None, ALU.mult).then_inc(top_found, 1)
            other = slots[:, :, 1, :]
            dve.match_replace(other, top8[:, :], spare, GONE).then_inc(replaced, 1)
            dve.wait_ge(exp_done, g + 1)
            own(dve)
            dve.reciprocal(stat[:, 2:3], stat[:, 1:2]).then_inc(inverse, 1)
            dve.wait_ge(replaced, g + 1)
            own(dve)

            def keep_top(z):
                dve.scalar_tensor_tensor(out=spare[:, z], in0=other[:, z], scalar=GONE / 2, in1=whole(2 * g)[:, z],
                                         op0=ALU.is_lt, op1=ALU.mult).then_inc(kept_top, 1)

            def scale(z):
                dve.wait_ge(kept_top, g * 2 + (z + 1))
                if z == 0:
                    dve.wait_ge(inverse, g + 1)
                own(dve)
                dve.tensor_scalar(spare[:, z], spare[:, z], stat[:, 2:3], None, ALU.mult).then_inc(prob_ready, 1)

            keep_top(0)
            scale(0)
            sums_stored(dve, g)
            for c in range(0, NTC, 2):
                take_transposed(dve, g, c, lambda o, a: dve.tensor_copy(o, a))
                if c == 0:
                    keep_top(1)
                if c == 2:
                    scale(1)

        def split_low(dve, l, h, line, after):
            dve.wait_ge(hi[l][h], after)
            dve.wait_ge(state[l][h], after)
            own(dve)
            dve.tensor_tensor(line_pairs(h, 1), line, line_pairs(h, 0), ALU.subtract).then_inc(lo[l][h], 1)

        def dve_rows(dve, l, k):
            target = shape_of(k)[3]

            def step(s, banks):
                at = target(s) if isinstance(s, int) else dve.snap(target(s))
                for h in range(2):
                    acc = banks[h][:, 0:HB * WP].rearrange("p (b j) -> p b j", b=HB)
                    line = rows_view(ALL, h)[:, 1:1 + HB, ds(at, 1), :].rearrange("p b r j -> p b (r j)")
                    dve.wait_ge(conv[l][h], s + (STEPS0[k] + 1))
                    own(dve)
                    dve.scalar_tensor_tensor(out=line_pairs(h, 0), in0=acc, scalar=0.0, in1=line, op0=ALU.max, op1=ALU.add
                                             ).then_inc(hi[l][h], 1)
                    dve.scalar_tensor_tensor(out=line, in0=acc, scalar=0.0, in1=line, op0=ALU.max, op1=ALU.add
                                             ).then_inc(state[l][h], 1)
                    split_low(dve, l, h, line, s + (LINES0[k] + 1))

            each_step(dve, k, step)

        def dve_columns(dve, l, k):
            view, s0, _, target, pairs = shape_of(k)
            with dve.Fori(0, STEPS[k]) as s:
                at = dve.snap(target(s))
                for h in range(2):
                    acc = PS[h][:, 0:HB * pairs].rearrange("p (b j) -> p b j", b=HB)
                    line = view(ALL, h)[:, s0:s0 + HB, ds(at, 1), :].rearrange("p b r j -> p b (r j)")
                    dve.wait_ge(conv[l][h], s + (STEPS0[k] + 1))
                    dve.scalar_tensor_tensor(out=line, in0=acc, scalar=0.0, in1=line, op0=ALU.max, op1=ALU.add
                                             ).then_inc(state[l][h], 1)

        def dve_layer(dve, l):
            dve.wait_ge(ln[2 * l].normed, NG * N2)
            for h in range(2):
                dve.sem_inc(state[l][h], 1)
            for h in range(2):
                for part in range(2):
                    for at in (0, EDGE + WP):
                        dve.tensor_copy(split_line(h, part)[:, :, at:at + EDGE],
                                        pick[:, 0:HB * EDGE].rearrange("p (b j) -> p b j", b=HB))
                line = rows_view(ALL, h)[:, 1:1 + HB, 0, :]
                dve.tensor_copy(line_pairs(h, 0), line).then_inc(hi[l][h], 1)
                split_low(dve, l, h, line, 1)
            dve.wait_ge(taps_hi[l], 1)
            dve.tensor_tensor(taps_part[1], taps[:, 0:2 * NO * 128], taps_part[0], ALU.subtract).then_inc(taps_lo[l], 1)
            dve_rows(dve, l, 0)
            dve_rows(dve, l, 1)
            relayout(dve, l, 0, lambda o, a: dve.tensor_copy(o, a))
            dve_columns(dve, l, 2)
            dve_columns(dve, l, 3)

        def bn_take(dve, u, k):
            g, d, v = u
            dve.wait_ge(ln[3].mixed, index(u, k + 1))
            dve.bn_stats(bns[:, ds(g * (N2 * 6) + (d * N2 + v * NCH + k) * 6, 6)], PS[5 + (v * NCH + k) % 2][:, 0:CH]
                         ).then_inc(ln[3].taken, 1)

        @block.vector
        def _(dve):
            dve.wait_ge(consts, 1)
            dve.tensor_tensor(centre[:, :], ident[:, :], average[:, :], ALU.subtract).then_inc(centre_ready, 1)
            dve.wait_ge(gate_t, 1)
            for v in range(2):
                for h in range(2):
                    c0 = v * 128 + v * 64 + h * E
                    last = dve.tensor_copy(half(gate, h)[:, c0:c0 + E], PS[7][0:C, 0:E])
            last.then_inc(gate_ready, 1)
            dve.wait_ge(rnn_t, 1)
            for h in range(2):
                dve.tensor_copy(half(wbd, h)[:, h * 64:(h + 1) * 64], PS[7][0:64, 64:128])
            dve.tensor_copy(vt[0:64, :], PS[7][0:64, 128:192]).then_inc(rnn_w_ready, 1)
            dve_taps(dve, 0)
            dve_norm(dve, 0)
            dve_layer(dve, 0)
            dve_norm(dve, 1, ending=lambda g: dve_route(dve, g))
            dve_taps(dve, 1)
            dve.wait_ge(eo_mm, 1)
            dve.tensor_copy(outt, PS[2][0:64, :]).then_inc(outt_ready, 1)
            dve.wait_ge(lh_zero, 1)
            dve.wait_ge(lh_tr, 1)
            for g in range(NG):
                for v in range(2):
                    for h in range(2):
                        p, c0 = v * 64 + h * E, (2 * g + v) * 128 + h * 64
                        last = dve.tensor_copy(lh[p:p + E, c0:c0 + 64], PS[3][p:p + E, g * 64:(g + 1) * 64])
            last.then_inc(lh_ready, 1)
            dve_norm(dve, 2)
            dve_layer(dve, 1)
            dve_norm(dve, 3, later=lambda u, k: bn_take(dve, u, k))

            def link(ins, n):
                ins.then_inc(bn_step, 1)
                dve.wait_ge(bn_step, n)
            dve.wait_ge(ln[3].taken, NG * N2)
            dve.bn_aggr(bnm[:, 0:2], bns[:, :]).then_inc(bn_dve, 1)
            dve.wait_ge(bn_pe, 1)
            link(dve.tensor_tensor(bnm[:, 2:3], bnm[:, 0:1], PS[7][:, 0:1], ALU.subtract), 1)
            dve.scalar_tensor_tensor(out=bnm[:, 3:4], in0=bnm[:, 2:3], scalar=bnm[:, 2:3], in1=bnm[:, 1:2],
                                     op0=ALU.mult, op1=ALU.add).then_inc(bn_dve, 1)
            dve.wait_ge(bn_std, 1)
            link(dve.reciprocal(bnm[0:64, 5:6], bnm[0:64, 4:5]), 2)
            link(dve.tensor_tensor(bnm[0:64, 6:7], bnm[0:64, 5:6], gb[:, 0:1], ALU.mult), 3)
            link(dve.tensor_tensor(bnm[0:64, 7:8], PS[7][0:64, 0:1], bnm[0:64, 6:7], ALU.mult), 4)
            link(dve.tensor_tensor(bnm[0:64, 8:9], gb[:, 1:2], bnm[0:64, 7:8], ALU.subtract), 5)
            dve.tensor_scalar(wrow, wraw_r[:, 0:64], bnm[0:64, 6:7], None, ALU.mult).then_inc(bn_dve, 1)
            for h in range(2):
                link(dve.memset(wsc[h], 0.0), 6 + h)
            link(dve.memset(yb[64:65], 1.0), 8)
            dve.memset(yb[0:64, BODY - 1, :, SEG - 1], 0.0).then_inc(step_y, BODY * SEG)
            dve.wait_ge(bn_pe, 3)
            for h in range(2):
                dve.tensor_copy(half(wsc[h], h), PS[7][0:64, 64:128])
            dve.tensor_copy(vt[64:65, :], PS[7][0:1, 128:192]).then_inc(rnn_ready, 1)
            dve.sem_inc(added, BODY)
            dve.sem_inc(out_st, 16)
            with dve.Fori(0, NIT) as i:
                dve.wait_ge(x2_in, i * 16 + 16)
                dve.wait_ge(out_st, i * 16 + 16)
                for s in range(BODY):
                    dve.wait_ge(seg_done, i * BODY + (s + 2))
                    dve.tensor_tensor(ob[:, :, s * SEG:(s + 1) * SEG], x2b[:, :, s * SEG:(s + 1) * SEG], yb[0:64, s, :, :],
                                      ALU.add).then_inc(added, 1)


_INS = ['x', 'L0_conv_w_d', 'L0_conv_w_u', 'L0_conv_w_r', 'L0_conv_w_l', 'L0_ffn_gate_w', 'L0_ffn_gate_b', 'L0_ffn_weight1',
        'L0_ffn_weight2', 'L1_conv_w_d', 'L1_conv_w_u', 'L1_conv_w_r', 'L1_conv_w_l', 'L1_ffn_W', 'L1_ffn_V', 'L1_ffn_gamma',
        'L1_ffn_beta']
_OUTS = [((B, C, H, W), 'float32')]


def kernel(**inputs):
    import numpy as _np
    import concourse.bacc as _bacc
    from concourse import mybir as _mybir
    from concourse.bass_utils import run_bass_kernel_spmd as _run

    nc = _bacc.Bacc("TRN2", target_bir_lowering=False, num_devices=1)
    arrays, a = {}, {}
    for name in _INS:
        v = _np.ascontiguousarray(inputs[name])
        arrays[f"in_{name}_dram"] = v
        a[name] = nc.dram_tensor(f"in_{name}_dram", v.shape, _mybir.dt.from_np(v.dtype), kind="ExternalInput").ap()
    outs = [nc.dram_tensor(f"out_{i}_dram", shape, _mybir.dt.from_np(_np.dtype(dtype)), kind="ExternalOutput").ap()
            for i, (shape, dtype) in enumerate(_OUTS)]
    scratch = [nc.dram_tensor(f"{n}_dram", (B, C, S), _mybir.dt.float32, kind="Internal").ap() for n in ("t", "x1", "x2")]
    metaformer(nc, a['x'], [a[f"L{l}_conv_w_{d}"] for l in range(2) for d in "durl"], a['L0_ffn_gate_w'], a['L0_ffn_gate_b'],
               a['L0_ffn_weight1'], a['L0_ffn_weight2'], a['L1_ffn_W'], a['L1_ffn_V'], a['L1_ffn_gamma'], a['L1_ffn_beta'],
               outs[0], *scratch)
    r = _run(nc, [arrays], core_ids=[0])
    return r.results[0]["out_0_dram"]
```
